# Optimizing a Trainium2 kernel written in Bass

```python
import numpy as np
import jax
import jax.numpy as jnp

def _softmax(x, axis=-1):
    return jax.nn.softmax(x, axis=axis)

def _gelu(x):
    return jax.nn.gelu(x, approximate=True)

def _silu(x):
    return jax.nn.silu(x)

def _sigmoid(x):
    return jax.nn.sigmoid(x)

def _layernorm(x, axis=-1, eps=1e-05):
    m = jnp.mean(x, axis=axis, keepdims=True)
    v = jnp.var(x, axis=axis, keepdims=True)
    return (x - m) / jnp.sqrt(v + eps)

def _scatter_add(tgt, idx, src, axis=0):
    return tgt.at[idx].add(src)

def _segment_sum(src, seg, n):
    return jax.ops.segment_sum(src, seg, n)
kernel_name = 'mk_dlrm_tower_d1_rec_r8_afcc7a'

def setup_inputs(seed: int=0):
    np.random.seed(seed)
    _w = jnp.asarray

    def _rec_inputs():
        import jax
        import jax.numpy as jnp
        _tk = jax.random.key(seed)
        dense_ctx = jax.random.normal(jax.random.fold_in(_tk, 190), (512, 16), jnp.float32)
        ids = jnp.stack([jax.random.randint(jax.random.fold_in(_tk, 200 + f), (512,), 0, v, jnp.int32) for f, v in enumerate([125000, 125000, 1250, 1250, 12500, 1000, 1250, 125000, 1000, 1000, 1000, 1250, 1250, 1250, 1250, 1250, 12500, 1000, 12500, 1000, 1250, 125000, 125000, 125000, 1250, 125000, 125000, 1000, 125000, 12500, 12500, 1000, 1250, 12500, 12500, 125000, 1250, 125000, 1250])], axis=1)
        tbl_0 = 0.05 * jax.random.normal(jax.random.fold_in(_tk, 500 + 0), (125000, 16), jnp.float32)
        tbl_1 = 0.05 * jax.random.normal(jax.random.fold_in(_tk, 500 + 1), (125000, 16), jnp.float32)
        tbl_2 = 0.05 * jax.random.normal(jax.random.fold_in(_tk, 500 + 2), (1250, 16), jnp.float32)
        tbl_3 = 0.05 * jax.random.normal(jax.random.fold_in(_tk, 500 + 3), (1250, 16), jnp.float32)
        tbl_4 = 0.05 * jax.random.normal(jax.random.fold_in(_tk, 500 + 4), (12500, 16), jnp.float32)
        tbl_5 = 0.05 * jax.random.normal(jax.random.fold_in(_tk, 500 + 5), (1000, 16), jnp.float32)
        tbl_6 = 0.05 * jax.random.normal(jax.random.fold_in(_tk, 500 + 6), (1250, 16), jnp.float32)
        tbl_7 = 0.05 * jax.random.normal(jax.random.fold_in(_tk, 500 + 7), (125000, 16), jnp.float32)
        tbl_8 = 0.05 * jax.random.normal(jax.random.fold_in(_tk, 500 + 8), (1000, 16), jnp.float32)
        tbl_9 = 0.05 * jax.random.normal(jax.random.fold_in(_tk, 500 + 9), (1000, 16), jnp.float32)
        tbl_10 = 0.05 * jax.random.normal(jax.random.fold_in(_tk, 500 + 10), (1000, 16), jnp.float32)
        tbl_11 = 0.05 * jax.random.normal(jax.random.fold_in(_tk, 500 + 11), (1250, 16), jnp.float32)
        tbl_12 = 0.05 * jax.random.normal(jax.random.fold_in(_tk, 500 + 12), (1250, 16), jnp.float32)
        tbl_13 = 0.05 * jax.random.normal(jax.random.fold_in(_tk, 500 + 13), (1250, 16), jnp.float32)
        tbl_14 = 0.05 * jax.random.normal(jax.random.fold_in(_tk, 500 + 14), (1250, 16), jnp.float32)
        tbl_15 = 0.05 * jax.random.normal(jax.random.fold_in(_tk, 500 + 15), (1250, 16), jnp.float32)
        tbl_16 = 0.05 * jax.random.normal(jax.random.fold_in(_tk, 500 + 16), (12500, 16), jnp.float32)
        tbl_17 = 0.05 * jax.random.normal(jax.random.fold_in(_tk, 500 + 17), (1000, 16), jnp.float32)
        tbl_18 = 0.05 * jax.random.normal(jax.random.fold_in(_tk, 500 + 18), (12500, 16), jnp.float32)
        tbl_19 = 0.05 * jax.random.normal(jax.random.fold_in(_tk, 500 + 19), (1000, 16), jnp.float32)
        tbl_20 = 0.05 * jax.random.normal(jax.random.fold_in(_tk, 500 + 20), (1250, 16), jnp.float32)
        tbl_21 = 0.05 * jax.random.normal(jax.random.fold_in(_tk, 500 + 21), (125000, 16), jnp.float32)
        tbl_22 = 0.05 * jax.random.normal(jax.random.fold_in(_tk, 500 + 22), (125000, 16), jnp.float32)
        tbl_23 = 0.05 * jax.random.normal(jax.random.fold_in(_tk, 500 + 23), (125000, 16), jnp.float32)
        tbl_24 = 0.05 * jax.random.normal(jax.random.fold_in(_tk, 500 + 24), (1250, 16), jnp.float32)
        tbl_25 = 0.05 * jax.random.normal(jax.random.fold_in(_tk, 500 + 25), (125000, 16), jnp.float32)
        tbl_26 = 0.05 * jax.random.normal(jax.random.fold_in(_tk, 500 + 26), (125000, 16), jnp.float32)
        tbl_27 = 0.05 * jax.random.normal(jax.random.fold_in(_tk, 500 + 27), (1000, 16), jnp.float32)
        tbl_28 = 0.05 * jax.random.normal(jax.random.fold_in(_tk, 500 + 28), (125000, 16), jnp.float32)
        tbl_29 = 0.05 * jax.random.normal(jax.random.fold_in(_tk, 500 + 29), (12500, 16), jnp.float32)
        tbl_30 = 0.05 * jax.random.normal(jax.random.fold_in(_tk, 500 + 30), (12500, 16), jnp.float32)
        tbl_31 = 0.05 * jax.random.normal(jax.random.fold_in(_tk, 500 + 31), (1000, 16), jnp.float32)
        tbl_32 = 0.05 * jax.random.normal(jax.random.fold_in(_tk, 500 + 32), (1250, 16), jnp.float32)
        tbl_33 = 0.05 * jax.random.normal(jax.random.fold_in(_tk, 500 + 33), (12500, 16), jnp.float32)
        tbl_34 = 0.05 * jax.random.normal(jax.random.fold_in(_tk, 500 + 34), (12500, 16), jnp.float32)
        tbl_35 = 0.05 * jax.random.normal(jax.random.fold_in(_tk, 500 + 35), (125000, 16), jnp.float32)
        tbl_36 = 0.05 * jax.random.normal(jax.random.fold_in(_tk, 500 + 36), (1250, 16), jnp.float32)
        tbl_37 = 0.05 * jax.random.normal(jax.random.fold_in(_tk, 500 + 37), (125000, 16), jnp.float32)
        tbl_38 = 0.05 * jax.random.normal(jax.random.fold_in(_tk, 500 + 38), (1250, 16), jnp.float32)
        _rk = jax.random.fold_in(_tk, 7)
        W_top1 = 0.05 * jax.random.normal(jax.random.fold_in(_tk, 801), (400, 512), jnp.float32)
        W_top2 = 0.0441942 * jax.random.normal(jax.random.fold_in(_tk, 802), (512, 256), jnp.float32)
        W_top3 = 0.0625 * jax.random.normal(jax.random.fold_in(_tk, 803), (256, 1), jnp.float32)
        b_top1 = jnp.zeros((512,), jnp.float32)
        b_top2 = jnp.zeros((256,), jnp.float32)
        return (dense_ctx, ids, tbl_0, tbl_1, tbl_2, tbl_3, tbl_4, tbl_5, tbl_6, tbl_7, tbl_8, tbl_9, tbl_10, tbl_11, tbl_12, tbl_13, tbl_14, tbl_15, tbl_16, tbl_17, tbl_18, tbl_19, tbl_20, tbl_21, tbl_22, tbl_23, tbl_24, tbl_25, tbl_26, tbl_27, tbl_28, tbl_29, tbl_30, tbl_31, tbl_32, tbl_33, tbl_34, tbl_35, tbl_36, tbl_37, tbl_38, W_top1, b_top1, W_top2, b_top2, W_top3)
    dense_ctx, ids, tbl_0, tbl_1, tbl_2, tbl_3, tbl_4, tbl_5, tbl_6, tbl_7, tbl_8, tbl_9, tbl_10, tbl_11, tbl_12, tbl_13, tbl_14, tbl_15, tbl_16, tbl_17, tbl_18, tbl_19, tbl_20, tbl_21, tbl_22, tbl_23, tbl_24, tbl_25, tbl_26, tbl_27, tbl_28, tbl_29, tbl_30, tbl_31, tbl_32, tbl_33, tbl_34, tbl_35, tbl_36, tbl_37, tbl_38, W_top1, b_top1, W_top2, b_top2, W_top3 = _rec_inputs()

    def _L0_rec_setup():
        import jax, jax.numpy as jnp
        import numpy as np
        B, F0, D = (512, 39, 16)
        CIN = [128, 128, 128]

        def _cin_layer(X0, Xi, W, b):
            H = W.shape[0]
            F0_, Fi = (X0.shape[1], Xi.shape[1])
            Wr = W.reshape(H, F0_, Fi)
            return jnp.einsum('hjk,bjd,bkd->bhd', Wr, X0, Xi) + b[None, :, None]
        key = jax.random.key(seed)
        ks = jax.random.split(key, 4)
        x = jax.random.normal(ks[0], (B, F0, D), dtype=jnp.float32)
        fields = [F0] + CIN
        inp = {'embedded_features': x}
        for i in range(len(CIN)):
            cin = F0 * fields[i]
            cout = fields[i + 1]
            kw = jax.random.fold_in(ks[1], i)
            inp[f'W{i}'] = jax.random.normal(kw, (cout, cin), dtype=jnp.float32) / np.sqrt(cin)
            inp[f'b{i}'] = jnp.zeros((cout,), dtype=jnp.float32)
        return inp
    _L0_rec_all = _L0_rec_setup()
    _L0_rec_in = {k: v for k, v in _L0_rec_all.items() if k in ('W0', 'b0', 'W1', 'b1', 'W2', 'b2')}
    del _L0_rec_all
    return {'dense_ctx': dense_ctx, 'ids': ids, 'tbl_0': tbl_0, 'tbl_1': tbl_1, 'tbl_2': tbl_2, 'tbl_3': tbl_3, 'tbl_4': tbl_4, 'tbl_5': tbl_5, 'tbl_6': tbl_6, 'tbl_7': tbl_7, 'tbl_8': tbl_8, 'tbl_9': tbl_9, 'tbl_10': tbl_10, 'tbl_11': tbl_11, 'tbl_12': tbl_12, 'tbl_13': tbl_13, 'tbl_14': tbl_14, 'tbl_15': tbl_15, 'tbl_16': tbl_16, 'tbl_17': tbl_17, 'tbl_18': tbl_18, 'tbl_19': tbl_19, 'tbl_20': tbl_20, 'tbl_21': tbl_21, 'tbl_22': tbl_22, 'tbl_23': tbl_23, 'tbl_24': tbl_24, 'tbl_25': tbl_25, 'tbl_26': tbl_26, 'tbl_27': tbl_27, 'tbl_28': tbl_28, 'tbl_29': tbl_29, 'tbl_30': tbl_30, 'tbl_31': tbl_31, 'tbl_32': tbl_32, 'tbl_33': tbl_33, 'tbl_34': tbl_34, 'tbl_35': tbl_35, 'tbl_36': tbl_36, 'tbl_37': tbl_37, 'tbl_38': tbl_38, 'W_top1': W_top1, 'b_top1': b_top1, 'W_top2': W_top2, 'b_top2': b_top2, 'W_top3': W_top3, 'L0_rec_W0': _L0_rec_in['W0'], 'L0_rec_b0': _L0_rec_in['b0'], 'L0_rec_W1': _L0_rec_in['W1'], 'L0_rec_b1': _L0_rec_in['b1'], 'L0_rec_W2': _L0_rec_in['W2'], 'L0_rec_b2': _L0_rec_in['b2']}

def reference(dense_ctx, ids, tbl_0, tbl_1, tbl_2, tbl_3, tbl_4, tbl_5, tbl_6, tbl_7, tbl_8, tbl_9, tbl_10, tbl_11, tbl_12, tbl_13, tbl_14, tbl_15, tbl_16, tbl_17, tbl_18, tbl_19, tbl_20, tbl_21, tbl_22, tbl_23, tbl_24, tbl_25, tbl_26, tbl_27, tbl_28, tbl_29, tbl_30, tbl_31, tbl_32, tbl_33, tbl_34, tbl_35, tbl_36, tbl_37, tbl_38, W_top1, b_top1, W_top2, b_top2, W_top3, L0_rec_W0, L0_rec_b0, L0_rec_W1, L0_rec_b1, L0_rec_W2, L0_rec_b2):
    import jax
    import jax.numpy as jnp

    def _L0_rec_ref(embedded_features, W0, b0, W1, b1, W2, b2):
        import jax, jax.numpy as jnp
        import numpy as np
        B, F0, D = (512, 39, 16)
        CIN = [128, 128, 128]

        def _cin_layer(X0, Xi, W, b):
            H = W.shape[0]
            F0_, Fi = (X0.shape[1], Xi.shape[1])
            Wr = W.reshape(H, F0_, Fi)
            return jnp.einsum('hjk,bjd,bkd->bhd', Wr, X0, Xi) + b[None, :, None]
        X0 = embedded_features
        Ws = [(W0, b0), (W1, b1), (W2, b2)]
        Xi = X0
        res = []
        for W, b in Ws:
            Xi = _cin_layer(X0, Xi, W, b)
            res.append(Xi.sum(axis=2))
        return jnp.concatenate(res, axis=1)
    e = jnp.stack([tbl_0[ids[:, 0]], tbl_1[ids[:, 1]], tbl_2[ids[:, 2]], tbl_3[ids[:, 3]], tbl_4[ids[:, 4]], tbl_5[ids[:, 5]], tbl_6[ids[:, 6]], tbl_7[ids[:, 7]], tbl_8[ids[:, 8]], tbl_9[ids[:, 9]], tbl_10[ids[:, 10]], tbl_11[ids[:, 11]], tbl_12[ids[:, 12]], tbl_13[ids[:, 13]], tbl_14[ids[:, 14]], tbl_15[ids[:, 15]], tbl_16[ids[:, 16]], tbl_17[ids[:, 17]], tbl_18[ids[:, 18]], tbl_19[ids[:, 19]], tbl_20[ids[:, 20]], tbl_21[ids[:, 21]], tbl_22[ids[:, 22]], tbl_23[ids[:, 23]], tbl_24[ids[:, 24]], tbl_25[ids[:, 25]], tbl_26[ids[:, 26]], tbl_27[ids[:, 27]], tbl_28[ids[:, 28]], tbl_29[ids[:, 29]], tbl_30[ids[:, 30]], tbl_31[ids[:, 31]], tbl_32[ids[:, 32]], tbl_33[ids[:, 33]], tbl_34[ids[:, 34]], tbl_35[ids[:, 35]], tbl_36[ids[:, 36]], tbl_37[ids[:, 37]], tbl_38[ids[:, 38]]], axis=1)
    z = _L0_rec_ref(e, L0_rec_W0, L0_rec_b0, L0_rec_W1, L0_rec_b1, L0_rec_W2, L0_rec_b2)
    z = z.reshape(z.shape[0], -1)
    h = jnp.concatenate([z, dense_ctx], axis=1)
    h = jnp.maximum(h @ W_top1 + b_top1, 0.0)
    h = jnp.maximum(h @ W_top2 + b_top2, 0.0)
    y = h @ W_top3
    return y

_drawn_inputs = setup_inputs


def setup_inputs(seed=0):
    import zlib

    import numpy as np

    out = dict(_drawn_inputs(seed))
    spreads = {'b_top1': (0.0, 0.1),
     'b_top2': (0.0, 0.1),
     'L0_rec_b0': (0.0, 0.1),
     'L0_rec_b1': (0.0, 0.1),
     'L0_rec_b2': (0.0, 0.1)}
    factors = {'tbl_0': 8.0,
     'tbl_1': 6.227,
     'tbl_2': 5.293,
     'tbl_3': 7.271,
     'tbl_4': 8.0,
     'tbl_5': 8.0,
     'tbl_6': 8.0,
     'tbl_7': 6.831,
     'tbl_8': 8.0,
     'tbl_9': 8.0,
     'tbl_10': 8.0,
     'tbl_11': 6.733,
     'tbl_12': 8.0,
     'tbl_13': 8.0,
     'tbl_14': 4.287,
     'tbl_15': 5.762,
     'tbl_16': 8.0,
     'tbl_17': 8.0,
     'tbl_18': 8.0,
     'tbl_19': 5.973,
     'tbl_20': 7.11,
     'tbl_21': 8.0,
     'tbl_22': 8.0,
     'tbl_23': 8.0,
     'tbl_24': 8.0,
     'tbl_25': 7.382,
     'tbl_26': 6.047,
     'tbl_27': 8.0,
     'tbl_28': 8.0,
     'tbl_29': 8.0,
     'tbl_30': 6.691,
     'tbl_31': 6.253,
     'tbl_32': 8.0,
     'tbl_33': 6.674,
     'tbl_34': 8.0,
     'tbl_35': 7.776,
     'tbl_36': 8.0,
     'tbl_37': 6.761,
     'tbl_38': 8.0,
     'L0_rec_W0': 3.219}
    for name, (base, spread) in spreads.items():
        noise = np.random.default_rng([zlib.crc32(name.encode()), seed]).standard_normal(out[name].shape)
        drawn = base * np.exp(spread * noise) if base else spread * noise
        out[name] = jnp.asarray(drawn.astype(out[name].dtype))
    for name, factor in factors.items():
        out[name] = (out[name] * factor).astype(out[name].dtype)
    return out
```

```python
from contextlib import ExitStack

import concourse.bass as bass
from concourse import mybir

F32 = mybir.dt.float32
F32R = mybir.dt.float32r
I32 = mybir.dt.int32
ALU = mybir.AluOpType
ACT = mybir.ActivationFunctionType
AX = mybir.AxisListType

P = 128
BATCH, FIELDS, DIM, HID = 512, 39, 16, 128
CTX = 16
TOP1, TOP2 = 512, 256

TILE_B = P // DIM
TILES = 4
GROUP_B = TILE_B * TILES
GROUP_N = P * TILES
GROUPS = BATCH // GROUP_B
BLOCKS = BATCH // P
BLOCK_G = GROUPS // BLOCKS
NT = GROUPS * TILES

REPS, CHUNKS = 3, 7
ROWS = REPS * FIELDS
LAST_ROWS = 2 * FIELDS
HALF = (FIELDS - 1) // 2

BANK_F = 4
BANKS = -(-FIELDS // BANK_F)
LAST_F = FIELDS - BANK_F * (BANKS - 1)
RING = 5
GRAM = FIELDS + 1

ACT_SCALES = (1, 3, 5, 7, 9)
DVE_SCALES = (0, 2, 4, 6, 8)
POOL_SUMS = ((1, 3), (5,), (7,))
DVE_SUMS = ((0, 2), (4,), (6,), (8,))
N_ACT, N_DVE = len(ACT_SCALES), len(DVE_SCALES)
PRODUCTS = TILES * N_ACT
assert N_ACT == N_DVE
N_POOL_SUM, N_CHAIN, N_TAIL = len(POOL_SUMS), len(DVE_SUMS), 4


def fields_of(m):
    return BANK_F if m < BANKS - 1 else LAST_F


def tower(nc, dense_ctx, ids, tables, W_top1, b_top1, W_top2, b_top2, W_top3,
          W0, b0, W1, b1, W2, b2, out):
    ctx = ExitStack()
    with ctx:
        def sb(name, shape, dt=F32):
            return ctx.enter_context(nc.sbuf_tensor(name, shape, dt))

        def pb(name):
            return ctx.enter_context(nc.psum_tensor(name, [P, 512], F32))

        def sem(name):
            return ctx.enter_context(nc.semaphore(name))

        ident = sb("ident", [P, P])
        mask = sb("mask", [P, TILE_B])
        idx = sb("idx", [P, FIELDS], I32)
        emb = sb("emb", [P, FIELDS, DIM])
        embt = sb("embt", [P, DIM, ROWS])
        x0t = [sb(f"x0t{u}", [P, TILES, ROWS]) for u in range(2)]
        x0r = sb("x0r", [ROWS, GROUP_N])
        late = sb("late", [P, CHUNKS * GROUP_N])
        x1h = [sb(f"x1h{u}", [P, GROUP_N], F32R) for u in range(2)]
        x1l = [sb(f"x1l{u}", [P, GROUP_N], F32R) for u in range(2)]
        w0t = sb("w0t", [ROWS, CHUNKS, HID])
        w1h = sb("w1h", [P, FIELDS * HID], F32R)
        w1l = sb("w1l", [P, FIELDS * HID], F32R)
        w2t = sb("w2t", [P, FIELDS, HID])
        prod = [sb(f"prod{m}", [P, BANK_F * HID]) for m in range(BANKS)]
        acc_d = [sb(f"acc_d{u}", [P, BANK_F * HID]) for u in range(2)]
        acc_p = [sb(f"acc_p{u}", [P, BANK_F * HID]) for u in range(2)]
        x2t = [sb(f"x2t{u}", [P, HID]) for u in range(2)]
        bdiag = [sb(f"bdiag{u}", [P, TILE_B, GRAM]) for u in range(2)]
        gram = sb("gram", [P, GRAM, BATCH])
        z0raw = sb("z0raw", [P, BATCH])
        b0c = sb("b0c", [P, 1])
        b2c = sb("b2c", [P, 1])
        b0s = sb("b0s", [P, 1])
        b2s = sb("b2s", [P, 1])
        wt3 = sb("wt3", [P, TOP2 // P])
        bt1 = sb("bt1", [P, TOP1 // P])
        bt2 = sb("bt2", [P, TOP2 // P])
        dctx = sb("dctx", [P, BLOCKS, CTX])
        yrow = x0r[0:1, :]

        flat = gram[:, :, :].rearrange("p c b -> p (c b)")
        w1raw = flat[:, 0:FIELDS * HID]
        w2raw = flat[:, 5120:5120 + FIELDS * HID]
        w0raw = flat[:, 10240:10240 + FIELDS * FIELDS]
        w0sym = flat[:, 12288:12288 + CHUNKS * ROWS]
        pairs = late[0:ROWS, :].rearrange("p (c n) -> p c n", c=CHUNKS)
        wt1 = late[:, 0:3 * TOP1].rearrange("p (c n) -> p c n", c=3)
        wt2 = late[:, 3 * TOP1:3 * TOP1 + TOP1 // P * TOP2].rearrange("p (c n) -> p c n", n=TOP2)
        wt1c = late[0:CTX, 5 * GROUP_N:6 * GROUP_N]
        dctxt = late[0:CTX, 6 * GROUP_N:7 * GROUP_N]
        z0s, z2s = prod[0], prod[1]
        h1 = [prod[2 + c] for c in range(TOP1 // P)]
        h2 = [prod[6 + c] for c in range(TOP2 // P)]

        yb = [pb(f"yb{i}") for i in range(RING)]
        p0 = pb("p0")
        pt = pb("pt")
        pg = pb("pg")

        ids_in = sem("ids_in")
        gathered = sem("gathered")
        embt_ready = sem("embt_ready")
        weights_in = sem("weights_in")
        w2_in = sem("w2_in")
        small_in = sem("small_in")
        b1_in = sem("b1_in")
        dense_in = sem("dense_in")
        consts = sem("consts")
        w0_sym = sem("w0_sym")
        w_turned = sem("w_turned")
        w_hi = sem("w_hi")
        w_lo = sem("w_lo")
        x0t_in = sem("x0t_in")
        x0_turned = sem("x0_turned")
        x0r_ready = sem("x0r_ready")
        rolled_in = [sem(f"rolled_in{c}") for c in range(CHUNKS)]
        pairs_ready = sem("pairs_ready")
        l0_done = sem("l0_done")
        x1h_ready = sem("x1h_ready")
        x1l_ready = sem("x1l_ready")
        z0_ready = sem("z0_ready")
        bank_ready = sem("bank_ready")
        act_scaled = sem("act_scaled")
        dve_scaled = sem("dve_scaled")
        pool_summed = sem("pool_summed")
        chain_summed = sem("chain_summed")
        tail_summed = sem("tail_summed")
        bdiag_ready = sem("bdiag_ready")
        gram_done = sem("gram_done")
        gram_copied = sem("gram_copied")
        z2_done = sem("z2_done")
        z_ready = sem("z_ready")
        ctx_turned = sem("ctx_turned")
        bias_ready = sem("bias_ready")
        h1_done = sem("h1_done")
        h1_ready = sem("h1_ready")
        h2_done = sem("h2_done")
        h2_ready = sem("h2_ready")
        y_done = sem("y_done")
        y_ready = sem("y_ready")
        y_out = sem("y_out")

        def wait_scaled(eng, T, m):
            if m in ACT_SCALES:
                eng.wait_ge(act_scaled, T * N_ACT + ACT_SCALES.index(m) + 1)
            else:
                eng.wait_ge(dve_scaled, T * N_DVE + DVE_SCALES.index(m) + 1)

        def wait_product_free(eng, T, m):
            for k, ms in enumerate(POOL_SUMS):
                if m in ms:
                    eng.wait_ge(pool_summed, T * N_POOL_SUM + k + 1)
            for k, ms in enumerate(DVE_SUMS):
                if m in ms:
                    eng.wait_ge(chain_summed, T * N_CHAIN + k + 1)
            if m == BANKS - 1:
                eng.wait_ge(tail_summed, T * N_TAIL + 1)

        def at_least(T, n):
            return not isinstance(T, int) or T >= n

        W_BANKS = -(-FIELDS // 4)
        W0_BANKS = -(-CHUNKS // 4)
        TURNS = W0_BANKS + 2 * W_BANKS

        block = ctx.enter_context(nc.Block())

        @block.sync
        def _(sp):
            sp.dma_start(idx[:, :], ids[0:P, :]).then_inc(ids_in, 16)
            sp.dma_start(w0raw, W0).then_inc(weights_in, 16)
            sp.dma_start(w1raw, W1).then_inc(weights_in, 16)
            sp.dma_start(w2raw, W2).then_inc(w2_in, 16)
            sp.dma_start(dctx[:, :, :], dense_ctx.rearrange("(c p) n -> p c n", p=P)).then_inc(small_in, 16)
            with nc.allow_non_contiguous_dma(reason="a few bias columns"):
                sp.dma_start(wt3[:, :], W_top3.rearrange("(c p) n -> p (c n)", p=P)).then_inc(small_in, 16)
                sp.dma_start(bt1[:, :], b_top1.rearrange("(c p) -> p c", p=P)).then_inc(small_in, 16)
                sp.dma_start(bt2[:, :], b_top2.rearrange("(c p) -> p c", p=P)).then_inc(small_in, 16)

            def chain(g, k):
                if at_least(g, 2):
                    sp.wait_ge(act_scaled, (g - 1) * PRODUCTS)
                    sp.wait_ge(dve_scaled, (g - 1) * PRODUCTS)
                    sp.wait_ge(bdiag_ready, (g - 1) * PRODUCTS)
                    if k == 0:
                        sp.wait_ge(embt_ready, (g - 1) * PRODUCTS)
                u = k % 2
                for t in range(TILES):
                    b = k * GROUP_B + t * TILE_B
                    sp.dma_start(x0t[u][:, t, :], embt[b:b + TILE_B, :, :]).then_inc(x0t_in, 16)
                sp.wait_ge(x0r_ready, g + 1)
                for c in range(CHUNKS):
                    for q in range(REPS if c < CHUNKS - 1 else REPS - 1):
                        s = c + CHUNKS * q
                        sp.dma_start(pairs[q * FIELDS:(q + 1) * FIELDS, c, :],
                                     x0r[s:s + FIELDS, :]).then_inc(rolled_in[c], 16)

            sp.wait_ge(embt_ready, 1)
            chain(0, 0)

            def rest_of_block(blk):
                sp.wait_ge(gathered, (blk + 1) * (16 * FIELDS))
                sp.dma_start(idx[:, :], ids[bass.ds(blk * P + P, P), :]).then_inc(ids_in, 16)
                for k in range(1, BLOCK_G):
                    chain(blk * BLOCK_G + k, k)
                chain(blk * BLOCK_G + BLOCK_G, 0)

            rest_of_block(0)
            with sp.Fori(1, BLOCKS - 1) as blk:
                rest_of_block(blk)
            for k in range(1, BLOCK_G):
                chain((BLOCKS - 1) * BLOCK_G + k, k)
            sp.wait_ge(l0_done, GROUPS)
            sp.dma_start(wt1, W_top1[0:3 * P, :].rearrange("(c p) n -> p c n", p=P)).then_inc(dense_in, 16)
            sp.dma_start(wt1c, W_top1[3 * P:3 * P + CTX, :]).then_inc(dense_in, 16)
            sp.dma_start(wt2, W_top2.rearrange("(c p) n -> p c n", p=P)).then_inc(dense_in, 16)
            sp.wait_ge(y_ready, 1)
            sp.dma_start(out.rearrange("b n -> n b"), yrow).then_inc(y_out, 16)
            sp.wait_ge(y_out, 16)

        @block.gpsimd
        def _(pool):
            def gather(j):
                pool.indirect_dma_start(emb[:, j, :], None, tables[j][:, :],
                                        bass.IndirectOffsetOnAxis(idx[:, j:j + 1], 0)).then_inc(gathered, 16)

            def permute(by):
                for r in range(REPS):
                    op = pool.tensor_copy(embt[:, :, r * FIELDS:(r + 1) * FIELDS],
                                          emb[:, :, :].rearrange("p j d -> p d j"))
                op.then_inc(embt_ready, by)

            pool.wait_ge(ids_in, 16)
            for j in range(FIELDS):
                gather(j)
            pool.memset(ident[:, :], 1.0).then_inc(consts, 1)
            pool.memset(mask[:, :], 1.0).then_inc(consts, 1)
            pool.wait_ge(consts, 1)
            pool.affine_select(out=ident[:, :], in_=ident[:, :], compare_op=ALU.is_equal, fill=0.0,
                               base=0, pattern=[[-1, P]], channel_multiplier=1).then_inc(consts, 1)
            pool.wait_ge(consts, 3)
            pool.affine_select(out=mask[:, :], in_=mask[:, :], compare_op=ALU.is_ge, fill=0.0,
                               base=0, pattern=[[-DIM, TILE_B]], channel_multiplier=1).then_inc(consts, 1)
            pool.wait_ge(consts, 4)
            pool.affine_select(out=mask[:, :], in_=mask[:, :], compare_op=ALU.is_ge, fill=0.0,
                               base=DIM - 1, pattern=[[DIM, TILE_B]], channel_multiplier=-1).then_inc(consts, 1)
            pool.wait_ge(consts, 5)
            for u in range(2):
                pool.tensor_copy(bdiag[u][:, :, FIELDS], mask[:, :]).then_inc(consts, 1)
            pool.wait_ge(gathered, 16 * FIELDS)
            permute(1)

            def tile(g, t, u):
                T = g * TILES + t
                if at_least(T, 2):
                    pool.wait_ge(gram_done, T - 1)
                pool.tensor_tensor(bdiag[t % 2][:, :, 0:FIELDS],
                                   mask[:, :, None].to_broadcast([P, TILE_B, FIELDS]),
                                   x0t[u][:, t, None, 0:FIELDS].to_broadcast([P, TILE_B, FIELDS]),
                                   ALU.mult).then_inc(bdiag_ready, N_ACT)

            def sums(g, t, k):
                T = g * TILES + t
                acc = acc_p[t % 2]
                for m in POOL_SUMS[k]:
                    wait_scaled(pool, T, m)
                if k == 0:
                    if at_least(T, 2):
                        pool.wait_ge(tail_summed, (T - 2) * N_TAIL + 2)
                    a, b = (prod[m][:, :] for m in POOL_SUMS[0])
                    pool.tensor_tensor(acc[:, :], a, b, ALU.add).then_inc(pool_summed, 1)
                else:
                    pool.wait_ge(pool_summed, T * N_POOL_SUM + k)
                    pool.tensor_tensor(acc[:, :], acc[:, :], prod[POOL_SUMS[k][0]][:, :],
                                       ALU.add).then_inc(pool_summed, 1)

            def period(g, k, todo, turn=None):
                todo = list(todo)
                share = -(-len(todo) // (TILES * N_POOL_SUM))
                pool.wait_ge(x0t_in, (g + 1) * (16 * TILES))
                if turn is not None:
                    pool.wait_ge(gathered, (turn + 1) * (16 * FIELDS))
                for t in range(TILES):
                    tile(g, t, k % 2)
                    if turn is not None and t == 0:
                        permute(BLOCK_G * PRODUCTS)
                    for s in range(N_POOL_SUM):
                        for _ in range(share):
                            if todo:
                                gather(todo.pop(0))
                        sums(g, t, s)

            each = -(-FIELDS // (BLOCK_G - 1))

            def whole_block(blk):
                pool.wait_ge(ids_in, (blk + 2) * 16)
                for k in range(BLOCK_G):
                    last = k == BLOCK_G - 1
                    todo = () if last else range(k * each, min(FIELDS, (k + 1) * each))
                    period(blk * BLOCK_G + k, k, todo, blk + 1 if last else None)

            whole_block(0)
            with pool.Fori(1, BLOCKS - 1) as blk:
                whole_block(blk)
            for k in range(BLOCK_G):
                period((BLOCKS - 1) * BLOCK_G + k, k, ())

        @block.scalar
        def _(act):
            with nc.allow_non_contiguous_dma(reason="a few bias columns"):
                act.dma_start(b0c[:, :], b0.rearrange("(p n) -> p n", n=1)).then_inc(small_in, 16)
                act.dma_start(b2c[:, :], b2.rearrange("(p n) -> p n", n=1)).then_inc(small_in, 16)
            act.dma_start(prod[BANKS - 1][:, LAST_F * HID:BANK_F * HID],
                          b1.rearrange("(a h) -> a h", a=1).to_broadcast([P, HID])).then_inc(b1_in, 16)

            for n in range(W0_BANKS + W_BANKS):
                act.wait_ge(w_turned, n + 1)
                if n < W0_BANKS:
                    for i in range(4 * n, min(4 * n + 4, CHUNKS)):
                        rows = ROWS if i < CHUNKS - 1 else LAST_ROWS
                        op = act.activation(w0t[0:rows, i, :], yb[n % RING][0:rows, (i % 4) * HID:(i % 4 + 1) * HID], ACT.Copy)
                    op.then_inc(w_hi, 1)
                else:
                    j = 4 * (n - W0_BANKS)
                    w = min(4, FIELDS - j) * HID
                    act.activation(w1h[:, j * HID:j * HID + w], yb[n % RING][:, 0:w], ACT.Copy).then_inc(w_hi, 1)
            act.wait_ge(small_in, 16 * 6)
            act.activation(b0s[:, :], b0c[:, :], ACT.Copy, scale=float(DIM)).then_inc(bias_ready, 1)
            act.activation(b2s[:, :], b2c[:, :], ACT.Copy, scale=float(DIM)).then_inc(bias_ready, 1)

            def copy_fields(g):
                act.wait_ge(x0_turned, g + 1)
                if at_least(g, 1):
                    act.wait_ge(pairs_ready, g * CHUNKS)
                act.activation(x0r[:, :], pt[0:ROWS, :], ACT.Copy).then_inc(x0r_ready, 1)

            def high_part(g, u):
                act.wait_ge(l0_done, g + 1)
                if at_least(g, 2):
                    act.wait_ge(bank_ready, (g - 1) * (TILES * BANKS))
                act.activation(x1h[u][:, :], p0[:, :], ACT.Identity, bias=b0c[:, :]).then_inc(x1h_ready, 1)

            def copy_gram(T):
                act.wait_ge(gram_done, T + 1)
                act.activation(gram[:, :, bass.ds(T * TILE_B, TILE_B)],
                               pg[:, 0:TILE_B * GRAM].rearrange("p (b c) -> p c b", c=GRAM),
                               ACT.Copy).then_inc(gram_copied, 1)

            def scale(g, t, u, m):
                T = g * TILES + t
                act.wait_ge(bank_ready, T * BANKS + m + 1)
                if at_least(T, 1):
                    wait_product_free(act, T - 1, m)
                for i in range(fields_of(m)):
                    j = BANK_F * m + i
                    op = act.activation(prod[m][:, i * HID:(i + 1) * HID], yb[m % RING][:, i * HID:(i + 1) * HID],
                                        ACT.Copy, scale=x0t[u][:, t, j:j + 1])
                op.then_inc(act_scaled, 1)

            def period(g, u, more):
                for t in range(TILES):
                    T = g * TILES + t
                    for n, m in enumerate(ACT_SCALES):
                        scale(g, t, u, m)
                        if n == 0 and t == 3 and more:
                            high_part(g + 1, 1 - u)
                        if n == 0 and t == 1 and more:
                            copy_fields(g + 1)
                        if n == 1 and at_least(T, 2):
                            copy_gram(T - 2)

            copy_fields(0)
            high_part(0, 0)
            period(0, 0, True)
            period(1, 1, True)
            with act.Fori(1, GROUPS // 2 - 1) as it:
                period(it * 2, 0, True)
                period(it * 2 + 1, 1, True)
            period(GROUPS - 2, 0, True)
            period(GROUPS - 1, 1, False)
            copy_gram(NT - 2)
            copy_gram(NT - 1)

            act.wait_ge(ctx_turned, 1)
            act.activation(dctxt, pt[0:CTX, :], ACT.Copy).then_inc(z_ready, 1)
            act.wait_ge(z0_ready, GROUPS)
            act.wait_ge(pool_summed, NT * N_POOL_SUM)
            act.wait_ge(tail_summed, NT * N_TAIL)
            act.activation(z0s[:, :], z0raw[:, :], ACT.Identity, bias=b0s[:, :]).then_inc(z_ready, 1)
            act.wait_ge(z2_done, 1)
            act.activation(z2s[:, :], p0[:, :], ACT.Identity, bias=b2s[:, :]).then_inc(z_ready, 1)
            for c in range(TOP1 // P):
                act.wait_ge(h1_done, c + 1)
                act.activation(h1[c][:, :], yb[c][:, :], ACT.Relu, bias=bt1[:, c:c + 1]).then_inc(h1_ready, 1)
            for c in range(TOP2 // P):
                act.wait_ge(h2_done, c + 1)
                act.activation(h2[c][:, :], (pt, pg)[c][:, :], ACT.Relu, bias=bt2[:, c:c + 1]).then_inc(h2_ready, 1)
            act.wait_ge(y_done, 1)
            act.activation(yrow, p0[0:1, :], ACT.Copy).then_inc(y_ready, 1)

        @block.vector
        def _(dve):
            dve.wait_ge(weights_in, 32)
            step = FIELDS + 1

            def cut(at, n):
                return w0raw[:, at:at + step * (n - 1) + 1:step]

            for s in range(HALF + 1):
                at = (s % CHUNKS) * ROWS + (s // CHUNKS) * FIELDS
                n = FIELDS - s
                if s == 0:
                    dve.tensor_copy(w0sym[:, at:at + FIELDS], cut(0, FIELDS)).then_inc(w0_sym, 1)
                else:
                    dve.tensor_tensor(w0sym[:, at:at + n], cut(s, n), cut(FIELDS * s, n), ALU.add).then_inc(w0_sym, 1)
                    dve.tensor_tensor(w0sym[:, at + n:at + FIELDS], cut(step * n + s - FIELDS, s),
                                      cut(step * n + FIELDS * (s - FIELDS), s), ALU.add).then_inc(w0_sym, 1)
            for n in range(W0_BANKS, TURNS):
                k = n - W0_BANKS
                j = 4 * (k % W_BANKS)
                w = min(4, FIELDS - j) * HID
                dve.wait_ge(w_turned, n + 1)
                if k < W_BANKS:
                    dve.wait_ge(w_hi, n + 1)
                    dve.tensor_tensor(w1l[:, j * HID:j * HID + w], yb[n % RING][:, 0:w],
                                      w1h[:, j * HID:j * HID + w].bitcast(F32), ALU.subtract).then_inc(w_lo, 1)
                else:
                    dve.tensor_copy(w2t[:, j:j + w // HID, :].rearrange("p j h -> p (j h)"),
                                    yb[n % RING][:, 0:w]).then_inc(w_lo, 1)

            def pair_chunk(g, c):
                rows = ROWS if c < CHUNKS - 1 else LAST_ROWS
                if c == 0:
                    dve.wait_ge(x0r_ready, g + 1)
                dve.wait_ge(rolled_in[c], (g + 1) * (16 * (rows // FIELDS)))
                dve.tensor_tensor(pairs[0:rows, c, :], pairs[0:rows, c, :], x0r[0:rows, :],
                                  ALU.mult).then_inc(pairs_ready, 1)

            def low_part(g, u):
                dve.wait_ge(x1h_ready, g + 1)
                dve.scalar_tensor_tensor(out=x1l[u][:, :], in0=p0[:, :], scalar=b0c[:, :],
                                         in1=x1h[u][:, :].bitcast(F32), op0=ALU.add,
                                         op1=ALU.subtract).then_inc(x1l_ready, 1)

            def sum_dims(g):
                dve.wait_ge(l0_done, g + 1)
                dve.tensor_reduce(z0raw[:, bass.ds(g * GROUP_B, GROUP_B)],
                                  p0[:, :].rearrange("p (b d) -> p b d", d=DIM), AX.X,
                                  ALU.add).then_inc(z0_ready, 1)

            def scale(g, t, u, m):
                T = g * TILES + t
                n = fields_of(m)
                dve.wait_ge(bank_ready, T * BANKS + m + 1)
                if at_least(T, 1):
                    wait_product_free(dve, T - 1, m)
                dve.tensor_tensor(prod[m][:, 0:n * HID].rearrange("p (j h) -> p j h", h=HID),
                                  yb[m % RING][:, 0:n * HID].rearrange("p (j h) -> p j h", h=HID),
                                  x0t[u][:, t, BANK_F * m:BANK_F * m + n, None].to_broadcast([P, n, HID]),
                                  ALU.mult).then_inc(dve_scaled, 1)

            def chain_sum(g, t, k):
                T = g * TILES + t
                acc = acc_d[t % 2]
                for m in DVE_SUMS[k]:
                    wait_scaled(dve, T, m)
                if k == 0:
                    if at_least(T, 2):
                        dve.wait_ge(tail_summed, (T - 1) * N_TAIL)
                    a, b = (prod[m][:, :] for m in DVE_SUMS[0])
                    dve.tensor_tensor(acc[:, :], a, b, ALU.add).then_inc(chain_summed, 1)
                else:
                    dve.wait_ge(chain_summed, T * N_CHAIN + k)
                    dve.tensor_tensor(acc[:, :], acc[:, :], prod[DVE_SUMS[k][0]][:, :],
                                      ALU.add).then_inc(chain_summed, 1)

            def tail_sum(T, p, k):
                acc = acc_d[p]
                if k == 0:
                    dve.wait_ge(chain_summed, (T + 1) * N_CHAIN)
                    wait_scaled(dve, T, BANKS - 1)
                    dve.tensor_tensor(acc[:, :], acc[:, :], prod[BANKS - 1][:, :], ALU.add).then_inc(tail_summed, 1)
                    return
                dve.wait_ge(tail_summed, T * N_TAIL + k)
                if k == 1:
                    dve.wait_ge(pool_summed, (T + 1) * N_POOL_SUM)
                    dve.tensor_tensor(acc[:, :], acc[:, :], acc_p[p][:, :], ALU.add).then_inc(tail_summed, 1)
                elif k == 2:
                    dve.tensor_tensor(acc[:, 0:2 * HID], acc[:, 0:2 * HID], acc[:, 2 * HID:4 * HID],
                                      ALU.add).then_inc(tail_summed, 1)
                else:
                    if at_least(T, 2):
                        dve.wait_ge(gram_done, T - 1)
                    dve.tensor_tensor(x2t[p][:, :], acc[:, 0:HID], acc[:, HID:2 * HID],
                                      ALU.add).then_inc(tail_summed, 1)

            def period(g, u, more):
                for t in range(TILES):
                    T = g * TILES + t
                    for n, m in enumerate(DVE_SCALES):
                        scale(g, t, u, m)
                        if n > 0:
                            chain_sum(g, t, n - 1)
                        if n < N_TAIL and at_least(T, 1):
                            tail_sum(T - 1, (t + 1) % 2, n)
                        if more:
                            if t == 1 and n >= 3:
                                pair_chunk(g + 1, n - 3)
                            if t == 2:
                                pair_chunk(g + 1, n + 2)
                            if t == 3 and n == 1:
                                low_part(g + 1, 1 - u)
                            if t == 3 and n == 2:
                                sum_dims(g + 1)

            for c in range(CHUNKS):
                pair_chunk(0, c)
            low_part(0, 0)
            sum_dims(0)
            dve.wait_ge(b1_in, 16)
            period(0, 0, True)
            period(1, 1, True)
            with dve.Fori(1, GROUPS // 2 - 1) as it:
                period(it * 2, 0, True)
                period(it * 2 + 1, 1, True)
            period(GROUPS - 2, 0, True)
            period(GROUPS - 1, 1, False)
            for k in range(N_TAIL):
                tail_sum(NT - 1, (NT - 1) % 2, k)

        @block.tensor
        def _(pe):
            pe.wait_ge(consts, 7)
            pe.wait_ge(w0_sym, 2 * HALF + 1)

            def wait_bank(n):
                if n < W0_BANKS + RING:
                    if n >= RING:
                        pe.wait_ge(w_hi, n - RING + 1)
                else:
                    pe.wait_ge(w_lo, n - RING - W0_BANKS + 1)

            for n in range(TURNS):
                if n >= RING:
                    wait_bank(n)
                if n == W0_BANKS + W_BANKS:
                    pe.wait_ge(w2_in, 16)
                if n < W0_BANKS:
                    for i in range(4 * n, min(4 * n + 4, CHUNKS)):
                        rows = ROWS if i < CHUNKS - 1 else LAST_ROWS
                        op = pe.transpose(yb[n % RING][0:rows, (i % 4) * HID:(i % 4 + 1) * HID],
                                          w0sym[:, i * ROWS:i * ROWS + rows], ident[:, :])
                else:
                    raw = w1raw if n < W0_BANKS + W_BANKS else w2raw
                    j0 = 4 * ((n - W0_BANKS) % W_BANKS)
                    for j in range(j0, min(j0 + 4, FIELDS)):
                        op = pe.transpose(yb[n % RING][:, (j - j0) * HID:(j - j0 + 1) * HID],
                                          raw[:, j * HID:(j + 1) * HID], ident[:, :])
                op.then_inc(w_turned, 1)

            def turn_fields(g, u):
                pe.wait_ge(x0t_in, (g + 1) * (16 * TILES))
                if at_least(g, 1):
                    pe.wait_ge(x0r_ready, g)
                for t in range(TILES):
                    op = pe.transpose(pt[0:ROWS, t * P:(t + 1) * P], x0t[u][:, t, :], ident[:, :])
                op.then_inc(x0_turned, 1)

            def layer0(g):
                if at_least(g, 1):
                    pe.wait_ge(x1h_ready, g)
                    pe.wait_ge(x1l_ready, g)
                    pe.wait_ge(z0_ready, g)
                for c in range(CHUNKS):
                    rows = ROWS if c < CHUNKS - 1 else LAST_ROWS
                    pe.wait_ge(pairs_ready, g * CHUNKS + c + 1)
                    op = pe.matmul(p0[:, :], w0t[0:rows, c, :], pairs[0:rows, c, :],
                                   start=(c == 0), stop=(c == CHUNKS - 1))
                op.then_inc(l0_done, 1)

            def gram_product(T, p):
                pe.wait_ge(tail_summed, (T + 1) * N_TAIL)
                pe.wait_ge(bdiag_ready, (T + 1) * N_ACT)
                if at_least(T, 1):
                    pe.wait_ge(gram_copied, T)
                pe.matmul(pg[:, 0:TILE_B * GRAM], x2t[p][:, :],
                          bdiag[p][:, :, :].rearrange("p b c -> p (b c)"),
                          start=True, stop=True).then_inc(gram_done, 1)

            def layer1_bank(g, t, u, m):
                T = g * TILES + t
                if m >= RING:
                    wait_scaled(pe, T, m - RING)
                elif at_least(T, 1):
                    wait_scaled(pe, T - 1, m + BANKS - RING)
                w = fields_of(m) * HID
                at = BANK_F * m * HID
                cols = slice(t * P, (t + 1) * P)
                hi, lo = x1h[u][:, cols], x1l[u][:, cols]
                pe.matmul(yb[m % RING][:, 0:w], hi, w1h[:, at:at + w], start=True, stop=False)
                pe.matmul(yb[m % RING][:, 0:w], hi, w1l[:, at:at + w], start=False, stop=False)
                pe.matmul(yb[m % RING][:, 0:w], lo, w1h[:, at:at + w], start=False,
                          stop=True).then_inc(bank_ready, 1)

            def period(g, u, more):
                pe.wait_ge(x1h_ready, g + 1)
                pe.wait_ge(x1l_ready, g + 1)
                for t in range(TILES):
                    T = g * TILES + t
                    for m in range(BANKS):
                        layer1_bank(g, t, u, m)
                        if m == 2 and at_least(T, 2):
                            gram_product(T - 2, t % 2)
                        if m == 6 and t == 0 and more:
                            turn_fields(g + 1, 1 - u)
                    if t == 2 and more:
                        layer0(g + 1)

            turn_fields(0, 0)
            pe.wait_ge(w_hi, W0_BANKS)
            layer0(0)
            pe.wait_ge(w_hi, W0_BANKS + W_BANKS)
            pe.wait_ge(w_lo, 2 * W_BANKS)
            period(0, 0, True)
            period(1, 1, True)
            with pe.Fori(1, GROUPS // 2 - 1) as it:
                period(it * 2, 0, True)
                period(it * 2 + 1, 1, True)
            period(GROUPS - 2, 0, True)
            period(GROUPS - 1, 1, False)
            pe.wait_ge(small_in, 16 * 6)
            pe.wait_ge(x0r_ready, GROUPS)
            for c in range(BLOCKS):
                op = pe.transpose(pt[0:CTX, c * P:(c + 1) * P], dctx[:, c, :], ident[:, :])
            op.then_inc(ctx_turned, 1)
            gram_product(NT - 2, 0)
            gram_product(NT - 1, 1)
            pe.wait_ge(gram_copied, NT)
            for j in range(FIELDS):
                op = pe.matmul(p0[:, :], w2t[:, j, :], gram[:, j, :], start=(j == 0), stop=(j == FIELDS - 1))
            op.then_inc(z2_done, 1)
            pe.wait_ge(z_ready, 2)
            pe.wait_ge(dense_in, 16 * 3)
            for c in range(TOP1 // P):
                wait_scaled(pe, NT - 1, BANKS - RING + c)
                cols = slice(c * P, (c + 1) * P)
                pe.matmul(yb[c][:, :], wt1[:, 0, cols], z0s[:, :], start=True, stop=False)
                pe.matmul(yb[c][:, :], wt1[:, 1, cols], gram[:, FIELDS, :], start=False, stop=False)
                pe.matmul(yb[c][:, :], wt1c[:, cols], dctxt, start=False, stop=False)
            pe.wait_ge(z_ready, 3)
            for c in range(TOP1 // P):
                pe.matmul(yb[c][:, :], wt1[:, 2, c * P:(c + 1) * P], z2s[:, :], start=False,
                          stop=True).then_inc(h1_done, 1)
            for c in range(TOP1 // P):
                pe.wait_ge(h1_ready, c + 1)
                for o in range(TOP2 // P):
                    op = pe.matmul((pt, pg)[o][:, :], wt2[:, c, o * P:(o + 1) * P], h1[c][:, :],
                                   start=(c == 0), stop=(c == TOP1 // P - 1))
                    if c == TOP1 // P - 1:
                        op.then_inc(h2_done, 1)
            for c in range(TOP2 // P):
                pe.wait_ge(h2_ready, c + 1)
                op = pe.matmul(p0[0:1, :], wt3[:, c:c + 1], h2[c][:, :], start=(c == 0), stop=(c == TOP2 // P - 1))
            op.then_inc(y_done, 1)


_TABLES = [f"tbl_{j}" for j in range(FIELDS)]
_REST = ["W_top1", "b_top1", "W_top2", "b_top2", "W_top3", "L0_rec_W0", "L0_rec_b0",
         "L0_rec_W1", "L0_rec_b1", "L0_rec_W2", "L0_rec_b2"]


def kernel(**inputs):
    import numpy as _np
    import concourse.bacc as _bacc
    from concourse import mybir as _mybir
    from concourse.bass_utils import run_bass_kernel_spmd as _run

    nc = _bacc.Bacc("TRN2", target_bir_lowering=False, num_devices=1,
                     dynamic_dma_scratch_size=8192)
    arrays, aps = {}, {}
    for name in ["dense_ctx", "ids"] + _TABLES + _REST:
        a = _np.ascontiguousarray(inputs[name])
        arrays[f"in_{name}_dram"] = a
        aps[name] = nc.dram_tensor(f"in_{name}_dram", a.shape, _mybir.dt.from_np(a.dtype),
                                   kind="ExternalInput").ap()
    out = nc.dram_tensor("out_0_dram", (BATCH, 1), _mybir.dt.float32, kind="ExternalOutput").ap()
    tower(nc, aps["dense_ctx"], aps["ids"], [aps[n] for n in _TABLES], *[aps[n] for n in _REST], out)
    r = _run(nc, [arrays], core_ids=[0])
    return r.results[0]["out_0_dram"]
```

```python
from contextlib import ExitStack

import concourse.bass as bass
from concourse import mybir

F32 = mybir.dt.float32
F32R = mybir.dt.float32r
I32 = mybir.dt.int32
ALU = mybir.AluOpType
ACT = mybir.ActivationFunctionType
AX = mybir.AxisListType

P = 128
BATCH, FIELDS, DIM, HID = 512, 39, 16, 128
CTX = 16
TOP1, TOP2 = 512, 256

TILE_B = P // DIM
TILES = 4
GROUP_B = TILE_B * TILES
GROUP_N = P * TILES
GROUPS = BATCH // GROUP_B
NT = GROUPS * TILES

QUARTERS = P // GROUP_B
PER_Q = -(-FIELDS // QUARTERS)
SHORT_Q = FIELDS - PER_Q * (QUARTERS - 1)
COLS = QUARTERS * PER_Q

REPS, CHUNKS = 3, 7
ROWS = REPS * FIELDS
LAST_ROWS = 2 * FIELDS
HALF = (FIELDS - 1) // 2

BANK_F = 4
BANKS = -(-FIELDS // BANK_F)
LAST_F = FIELDS - BANK_F * (BANKS - 1)
RING = 5
GRAM = FIELDS + 1

ACT_SCALES = (1, 2, 4, 6, 7, 9)
DVE_SCALES = (0, 3, 5, 8)
POOL_SUMS = ((1, 2), (4,), (6,))
DVE_SUMS = ((0, 3), (5,), (7,), (8,))
N_ACT, N_DVE = len(ACT_SCALES), len(DVE_SCALES)
N_POOL_SUM, N_CHAIN, N_TAIL = len(POOL_SUMS), len(DVE_SUMS), 4


CHAIN_AT = {4: 0, 6: 1, 8: 2}
LAST_CHAIN_AT = 0
TAIL_AT = {1: 0, 3: 1, 5: 2, 7: 3}
GRAM_AT = 2

PAIR_SLOTS = ((0, 6), (0, 8), (1, 2), (1, 6), (2, 0), (2, 4), (2, 8))
LAYER0_SLOTS = ((1, 1), (1, 4), (1, 7), (2, 1), (2, 5), (2, 8), (3, 3))
HIGH_SLOT, LOW_SLOT, Z0_SLOT = (3, 4), (3, 5), (3, 8)
DIMS_SLOT, THREE_SLOT, TURN_SLOT, COPY_SLOT = (2, 1), (3, 1), (3, 5), (3, 7)
GATHERS_AT_ONCE = 2
EARLY = 4


def fields_of(m):
    return BANK_F if m < BANKS - 1 else LAST_F


def tower(nc, dense_ctx, ids, table, bases, W_top1, b_top1, W_top2, b_top2, W_top3,
          W0, b0, W1, b1, W2, b2, out):
    ctx = ExitStack()
    with ctx:
        def sb(name, shape, dt=F32):
            return ctx.enter_context(nc.sbuf_tensor(name, shape, dt))

        def pb(name):
            return ctx.enter_context(nc.psum_tensor(name, [P, 512], F32))

        def sem(name):
            return ctx.enter_context(nc.semaphore(name))

        ident = sb("ident", [P, P])
        mask = sb("mask", [P, TILE_B])
        ids_all = sb("ids_all", [P, GROUPS, PER_Q], I32)
        base = sb("base", [P, PER_Q], I32)
        idx = [sb(f"idx{u}", [P, PER_Q], I32) for u in range(2)]
        emb = [sb(f"emb{u}", [P, PER_Q, DIM]) for u in range(2)]
        embq = [sb(f"embq{u}", [P, DIM, PER_Q]) for u in range(2)]
        embt = [sb(f"embt{u}", [GROUP_B, DIM, COLS]) for u in range(2)]
        x0t = [sb(f"x0t{u}", [P, TILES, COLS]) for u in range(2)]
        x0a = sb("x0a", [P, TILES, COLS])
        x0t3 = sb("x0t3", [P, TILES, ROWS])
        x0r = sb("x0r", [ROWS, GROUP_N])
        late = sb("late", [P, CHUNKS * GROUP_N])
        x1h = [sb(f"x1h{u}", [P, GROUP_N], F32R) for u in range(2)]
        x1l = [sb(f"x1l{u}", [P, GROUP_N], F32R) for u in range(2)]
        w0t = sb("w0t", [ROWS, CHUNKS, HID])
        w1h = sb("w1h", [P, FIELDS * HID], F32R)
        w1l = sb("w1l", [P, FIELDS * HID], F32R)
        w2t = sb("w2t", [P, FIELDS, HID])
        prod = [sb(f"prod{m}", [P, BANK_F * HID]) for m in range(BANKS)]
        acc_d = [sb(f"acc_d{u}", [P, BANK_F * HID]) for u in range(2)]
        acc_p = [sb(f"acc_p{u}", [P, BANK_F * HID]) for u in range(2)]
        x2t = [sb(f"x2t{u}", [P, HID]) for u in range(2)]
        bdiag = [sb(f"bdiag{u}", [P, TILE_B, GRAM]) for u in range(2)]
        gram = sb("gram", [P, GRAM, BATCH])
        z0raw = sb("z0raw", [P, BATCH])
        b0c = sb("b0c", [P, 1])
        b2c = sb("b2c", [P, 1])
        b0s = sb("b0s", [P, 1])
        b2s = sb("b2s", [P, 1])
        wt3 = sb("wt3", [P, TOP2 // P])
        bt1 = sb("bt1", [P, TOP1 // P])
        bt2 = sb("bt2", [P, TOP2 // P])
        dctx = sb("dctx", [P, BATCH // P, CTX])
        yrow = x0r[0:1, :]

        flat = gram[:, :, :].rearrange("p c b -> p (c b)")
        w1raw = flat[:, 0:FIELDS * HID]
        w2raw = flat[:, 5120:5120 + FIELDS * HID]
        w0raw = flat[:, 10240:10240 + FIELDS * FIELDS]
        w0sym = flat[:, 12288:12288 + CHUNKS * ROWS]
        pairs = late[0:ROWS, :].rearrange("p (c n) -> p c n", c=CHUNKS)
        wt1 = late[:, 0:3 * TOP1].rearrange("p (c n) -> p c n", c=3)
        wt2 = late[:, 3 * TOP1:3 * TOP1 + TOP1 // P * TOP2].rearrange("p (c n) -> p c n", n=TOP2)
        wt1c = late[0:CTX, 5 * GROUP_N:6 * GROUP_N]
        dctxt = late[0:CTX, 6 * GROUP_N:7 * GROUP_N]
        z0s, z2s = prod[0], prod[1]
        h1 = [prod[2 + c] for c in range(TOP1 // P)]
        h2 = [prod[6 + c] for c in range(TOP2 // P)]

        x0d = nc.dram_tensor("x0_scratch", [2, 2 * FIELDS, GROUP_N], F32, kind="Internal").ap()

        yb = [pb(f"yb{i}") for i in range(RING)]
        p0 = pb("p0")
        pt = pb("pt")
        pg = pb("pg")

        ids_in = sem("ids_in")
        idx_ready = sem("idx_ready")
        gathered = [sem(f"gathered{u}") for u in range(2)]
        embq_ready = sem("embq_ready")
        embt_in = sem("embt_in")
        weights_in = sem("weights_in")
        w2_in = sem("w2_in")
        small_in = sem("small_in")
        b1_in = sem("b1_in")
        dense_in = sem("dense_in")
        consts = sem("consts")
        w0_sym = sem("w0_sym")
        w_turned = sem("w_turned")
        w_hi = sem("w_hi")
        w_lo = sem("w_lo")
        sp_waited = sem("sp_waited")
        x0a_in = sem("x0a_in")
        x0t_in = [sem(f"x0t_in{u}") for u in range(2)]
        x0t3_ready = sem("x0t3_ready")
        x0_turned = sem("x0_turned")
        x0r_ready = sem("x0r_ready")
        x0d_out = sem("x0d_out")
        rolled_in = [sem(f"rolled_in{h}") for h in range(2)]
        pairs_ready = sem("pairs_ready")
        l0_done = sem("l0_done")
        x1h_ready = sem("x1h_ready")
        x1l_ready = sem("x1l_ready")
        z0_ready = sem("z0_ready")
        bank_ready = sem("bank_ready")
        act_scaled = sem("act_scaled")
        dve_scaled = sem("dve_scaled")
        pool_summed = sem("pool_summed")
        chain_summed = sem("chain_summed")
        tail_summed = sem("tail_summed")
        bdiag_ready = sem("bdiag_ready")
        gram_done = sem("gram_done")
        gram_copied = sem("gram_copied")
        z2_done = sem("z2_done")
        z_ready = sem("z_ready")
        ctx_turned = sem("ctx_turned")
        bias_ready = sem("bias_ready")
        h1_done = sem("h1_done")
        h1_ready = sem("h1_ready")
        h2_done = sem("h2_done")
        h2_ready = sem("h2_ready")
        y_done = sem("y_done")
        y_ready = sem("y_ready")
        y_out = sem("y_out")

        def wait_scaled(eng, T, m):
            if m in ACT_SCALES:
                eng.wait_ge(act_scaled, T * N_ACT + ACT_SCALES.index(m) + 1)
            else:
                eng.wait_ge(dve_scaled, T * N_DVE + DVE_SCALES.index(m) + 1)

        def wait_product_free(eng, T, m):
            for k, ms in enumerate(POOL_SUMS):
                if m in ms:
                    eng.wait_ge(pool_summed, T * N_POOL_SUM + k + 1)
            for k, ms in enumerate(DVE_SUMS):
                if m in ms:
                    eng.wait_ge(chain_summed, T * N_CHAIN + k + 1)
            if m == BANKS - 1:
                eng.wait_ge(tail_summed, T * N_TAIL + 1)

        def at_least(T, n):
            return not isinstance(T, int) or T >= n

        W_BANKS = -(-FIELDS // 4)
        W0_BANKS = -(-CHUNKS // 4)
        TURNS = W0_BANKS + 2 * W_BANKS

        block = ctx.enter_context(nc.Block())

        @block.sync
        def _(sp):
            sp.dma_start(base[:, :], bases).then_inc(ids_in, 16)
            for h in range(QUARTERS):
                n = PER_Q if h < QUARTERS - 1 else SHORT_Q
                sp.dma_start(ids_all[h * GROUP_B:(h + 1) * GROUP_B, :, 0:n],
                             ids[:, h * PER_Q:h * PER_Q + n].rearrange("(g b) i -> b g i", b=GROUP_B)).then_inc(ids_in, 16)
            sp.dma_start(w0raw, W0).then_inc(weights_in, 16)
            sp.dma_start(w1raw, W1).then_inc(weights_in, 16)
            sp.dma_start(w2raw, W2).then_inc(w2_in, 16)
            sp.dma_start(dctx[:, :, :], dense_ctx.rearrange("(c p) n -> p c n", p=P)).then_inc(small_in, 16)
            with nc.allow_non_contiguous_dma(reason="a few bias columns"):
                sp.dma_start(wt3[:, :], W_top3.rearrange("(c p) n -> p (c n)", p=P)).then_inc(small_in, 16)
                sp.dma_start(bt1[:, :], b_top1.rearrange("(c p) -> p c", p=P)).then_inc(small_in, 16)
                sp.dma_start(bt2[:, :], b_top2.rearrange("(c p) -> p c", p=P)).then_inc(small_in, 16)

            def samples(g, u):
                for h in range(QUARTERS):
                    sp.dma_start(embt[u][:, :, h * PER_Q:(h + 1) * PER_Q],
                                 embq[u][h * GROUP_B:(h + 1) * GROUP_B, :, :]).then_inc(embt_in, 16)

            def columns(dst, g, u, done):
                for t in range(TILES):
                    sp.dma_start(dst[:, t, :], embt[u][t * TILE_B:(t + 1) * TILE_B, :, :]).then_inc(done, 16)

            def rolled(g, u):
                sp.wait_ge(x0r_ready, g + 1)
                sp.dma_start(x0d[u, :, :], x0r[0:2 * FIELDS, :]).then_inc(x0d_out, 16)
                sp.wait_ge(x0d_out, (g + 1) * 16)
                for h, (c0, c1) in enumerate(((0, EARLY), (EARLY, CHUNKS))):
                    for q in range(REPS):
                        n = c1 - c0 - (1 if q == REPS - 1 and c1 == CHUNKS else 0)
                        first = x0d[u, c0 + CHUNKS * q:c0 + CHUNKS * q + FIELDS, :]
                        row = first.ap[0][0]
                        src = bass.AP(first.tensor, first.offset, [[row, FIELDS], [row, n], [1, GROUP_N]])
                        sp.dma_start(pairs[q * FIELDS:(q + 1) * FIELDS, c0:c0 + n, :], src).then_inc(rolled_in[h], 16)

            def prepare(g, u):
                sp.wait_ge(embq_ready, g + 1)
                samples(g, u)
                if at_least(g, 1):
                    sp.wait_ge(x0t3_ready, g)
                    sp.sem_inc(sp_waited, 1)
                sp.wait_ge(embt_in, (g + 1) * (16 * QUARTERS))
                columns(x0a, g, u, x0a_in)
                rolled(g, u)

            def period(g, u, more=2):
                if more > 0:
                    if at_least(g, 1):
                        sp.wait_ge(act_scaled, g * (TILES * N_ACT))
                        sp.sem_inc(sp_waited, 1)
                        sp.wait_ge(dve_scaled, g * (TILES * N_DVE))
                        sp.wait_ge(bdiag_ready, g * (TILES * N_DVE))
                    columns(x0t[1 - u], g + 1, 1 - u, x0t_in[1 - u])
                if more > 1:
                    prepare(g + 2, u)

            prepare(0, 0)
            columns(x0t[0], 0, 0, x0t_in[0])
            prepare(1, 1)
            period(0, 0)
            period(1, 1)
            with sp.Fori(1, GROUPS // 2 - 1) as it:
                period(it * 2, 0)
                period(it * 2 + 1, 1)
            period(GROUPS - 2, 0, 1)
            sp.wait_ge(l0_done, GROUPS)
            sp.dma_start(wt1, W_top1[0:3 * P, :].rearrange("(c p) n -> p c n", p=P)).then_inc(dense_in, 16)
            sp.dma_start(wt1c, W_top1[3 * P:3 * P + CTX, :]).then_inc(dense_in, 16)
            sp.dma_start(wt2, W_top2.rearrange("(c p) n -> p c n", p=P)).then_inc(dense_in, 16)
            sp.wait_ge(y_ready, 1)
            sp.dma_start(out.rearrange("b n -> n b"), yrow).then_inc(y_out, 16)
            sp.wait_ge(y_out, 16)

        @block.gpsimd
        def _(pool):
            def rows_of(g, u):
                pool.tensor_tensor(idx[u][:, 0:SHORT_Q], ids_all[:, g, 0:SHORT_Q] if isinstance(g, int) else
                                   ids_all[:, bass.ds(g, 1), 0:SHORT_Q].rearrange("p g i -> p (g i)"),
                                   base[:, 0:SHORT_Q], ALU.add).then_inc(idx_ready, 1)
                n = (QUARTERS - 1) * GROUP_B
                pool.tensor_tensor(idx[u][0:n, SHORT_Q:PER_Q], ids_all[0:n, g, SHORT_Q:PER_Q] if isinstance(g, int) else
                                   ids_all[0:n, bass.ds(g, 1), SHORT_Q:PER_Q].rearrange("p g i -> p (g i)"),
                                   base[0:n, SHORT_Q:PER_Q], ALU.add).then_inc(idx_ready, 1)

            def gather(u, i):
                n = P if i < SHORT_Q else (QUARTERS - 1) * GROUP_B
                pool.indirect_dma_start(emb[u][0:n, i, :], None, table[:, :],
                                        bass.IndirectOffsetOnAxis(idx[u][0:n, i:i + 1], 0)).then_inc(gathered[u], 16)

            for u in range(2):
                pool.memset(emb[u][:, :, :], 0.0).then_inc(consts, 1)
            pool.wait_ge(consts, 2)
            pool.wait_ge(ids_in, 16 * (1 + QUARTERS))
            for u in range(2):
                rows_of(u, u)
                pool.wait_ge(idx_ready, 2 * (u + 1))
                for i in range(PER_Q):
                    gather(u, i)
            pool.memset(ident[:, :], 1.0).then_inc(consts, 1)
            pool.memset(mask[:, :], 1.0).then_inc(consts, 1)
            pool.wait_ge(consts, 3)
            pool.affine_select(out=ident[:, :], in_=ident[:, :], compare_op=ALU.is_equal, fill=0.0,
                               base=0, pattern=[[-1, P]], channel_multiplier=1).then_inc(consts, 1)
            pool.wait_ge(consts, 5)
            pool.affine_select(out=mask[:, :], in_=mask[:, :], compare_op=ALU.is_ge, fill=0.0,
                               base=0, pattern=[[-DIM, TILE_B]], channel_multiplier=1).then_inc(consts, 1)
            pool.wait_ge(consts, 6)
            pool.affine_select(out=mask[:, :], in_=mask[:, :], compare_op=ALU.is_ge, fill=0.0,
                               base=DIM - 1, pattern=[[DIM, TILE_B]], channel_multiplier=-1).then_inc(consts, 1)
            pool.wait_ge(consts, 7)
            for u in range(2):
                pool.tensor_copy(bdiag[u][:, :, FIELDS], mask[:, :]).then_inc(consts, 1)

            def tile(g, t, u):
                T = g * TILES + t
                if at_least(T, 2):
                    pool.wait_ge(gram_done, T - 1)
                pool.tensor_tensor(bdiag[t % 2][:, :, 0:FIELDS],
                                   mask[:, :, None].to_broadcast([P, TILE_B, FIELDS]),
                                   x0t[u][:, t, None, 0:FIELDS].to_broadcast([P, TILE_B, FIELDS]),
                                   ALU.mult).then_inc(bdiag_ready, N_DVE)

            def sums(g, t, k):
                T = g * TILES + t
                acc = acc_p[t % 2]
                for m in POOL_SUMS[k]:
                    wait_scaled(pool, T, m)
                if k == 0:
                    if at_least(T, 2):
                        pool.wait_ge(tail_summed, (T - 2) * N_TAIL + 2)
                    a, b = (prod[m][:, :] for m in POOL_SUMS[0])
                    pool.tensor_tensor(acc[:, :], a, b, ALU.add).then_inc(pool_summed, 1)
                else:
                    pool.wait_ge(pool_summed, T * N_POOL_SUM + k)
                    pool.tensor_tensor(acc[:, :], acc[:, :], prod[POOL_SUMS[k][0]][:, :],
                                       ALU.add).then_inc(pool_summed, 1)

            def period(g, u, more):
                pool.wait_ge(x0t_in[u], (g + 2 - u) * (8 * TILES))
                todo = list(range(PER_Q)) if more else []
                if more:
                    pool.wait_ge(embq_ready, g + 1)
                for t in range(TILES):
                    tile(g, t, u)
                    if more and t == 0:
                        rows_of(g + 2, u)
                    for s in range(N_POOL_SUM):
                        if more and t == 0 and s == 0:
                            pool.wait_ge(idx_ready, 2 * (g + 3))
                        sums(g, t, s)
                        for i in todo[:GATHERS_AT_ONCE]:
                            gather(u, i)
                        del todo[:GATHERS_AT_ONCE]

            period(0, 0, True)
            period(1, 1, True)
            with pool.Fori(1, GROUPS // 2 - 1) as it:
                period(it * 2, 0, True)
                period(it * 2 + 1, 1, True)
            period(GROUPS - 2, 0, False)
            period(GROUPS - 1, 1, False)

        @block.scalar
        def _(act):
            with nc.allow_non_contiguous_dma(reason="a few bias columns"):
                act.dma_start(b0c[:, :], b0.rearrange("(p n) -> p n", n=1)).then_inc(small_in, 16)
                act.dma_start(b2c[:, :], b2.rearrange("(p n) -> p n", n=1)).then_inc(small_in, 16)
            act.dma_start(prod[BANKS - 1][:, LAST_F * HID:BANK_F * HID],
                          b1.rearrange("(a h) -> a h", a=1).to_broadcast([P, HID])).then_inc(b1_in, 16)

            for n in range(W0_BANKS + W_BANKS):
                act.wait_ge(w_turned, n + 1)
                if n < W0_BANKS:
                    for i in range(4 * n, min(4 * n + 4, CHUNKS)):
                        rows = ROWS if i < CHUNKS - 1 else LAST_ROWS
                        op = act.activation(w0t[0:rows, i, :], yb[n % RING][0:rows, (i % 4) * HID:(i % 4 + 1) * HID], ACT.Copy)
                    op.then_inc(w_hi, 1)
                else:
                    j = 4 * (n - W0_BANKS)
                    w = min(4, FIELDS - j) * HID
                    act.activation(w1h[:, j * HID:j * HID + w], yb[n % RING][:, 0:w], ACT.Copy).then_inc(w_hi, 1)
            act.wait_ge(small_in, 16 * 6)
            act.activation(b0s[:, :], b0c[:, :], ACT.Copy, scale=float(DIM)).then_inc(bias_ready, 1)
            act.activation(b2s[:, :], b2c[:, :], ACT.Copy, scale=float(DIM)).then_inc(bias_ready, 1)

            def copy_fields(g):
                act.wait_ge(x0_turned, g + 1)
                if at_least(g, 1):
                    act.wait_ge(pairs_ready, g * CHUNKS)
                act.activation(x0r[:, :], pt[0:ROWS, :], ACT.Copy).then_inc(x0r_ready, 1)

            def dims_outside(g, half_g, u):
                act.wait_ge(gathered[u], (half_g + 1) * (16 * PER_Q))
                if at_least(g, 2):
                    act.wait_ge(embt_in, (g - 1) * (16 * QUARTERS))
                act.activation(embq[u][:, :, :], emb[u][:, :, :].rearrange("p i d -> p d i"),
                               ACT.Copy).then_inc(embq_ready, 1)

            def three_times(g):
                act.wait_ge(x0a_in, (g + 1) * (16 * TILES))
                if at_least(g, 1):
                    act.wait_ge(x0_turned, g)
                act.activation(x0t3[:, :, :].rearrange("p t (r j) -> p t r j", r=REPS),
                               x0a[:, :, None, 0:FIELDS].to_broadcast([P, TILES, REPS, FIELDS]),
                               ACT.Copy).then_inc(x0t3_ready, 1)

            def high_part(g, u):
                act.wait_ge(l0_done, g + 1)
                if at_least(g, 2):
                    act.wait_ge(bank_ready, (g - 1) * (TILES * BANKS))
                act.activation(x1h[u][:, :], p0[:, :], ACT.Identity, bias=b0c[:, :]).then_inc(x1h_ready, 1)

            def copy_gram(T):
                act.wait_ge(gram_done, T + 1)
                act.activation(gram[:, :, bass.ds(T * TILE_B, TILE_B)],
                               pg[:, 0:TILE_B * GRAM].rearrange("p (b c) -> p c b", c=GRAM),
                               ACT.Copy).then_inc(gram_copied, 1)

            def scale(g, t, u, m):
                T = g * TILES + t
                if t == 0 and m == ACT_SCALES[0]:
                    act.wait_ge(x0t_in[u], (g + 2 - u) * (8 * TILES))
                act.wait_ge(bank_ready, T * BANKS + m + 1)
                if at_least(T, 1):
                    wait_product_free(act, T - 1, m)
                for i in range(fields_of(m)):
                    j = BANK_F * m + i
                    op = act.activation(prod[m][:, i * HID:(i + 1) * HID], yb[m % RING][:, i * HID:(i + 1) * HID],
                                        ACT.Copy, scale=x0t[u][:, t, j:j + 1])
                op.then_inc(act_scaled, 1)

            def period(g, half_g, u, more):
                for t in range(TILES):
                    T = g * TILES + t
                    for m in range(BANKS):
                        if m in ACT_SCALES:
                            scale(g, t, u, m)
                        if more > 0 and (t, m) == HIGH_SLOT:
                            high_part(g + 1, 1 - u)
                        if more > 1 and (t, m) == DIMS_SLOT:
                            dims_outside(g + 2, half_g + 1, u)
                        if more > 1 and (t, m) == THREE_SLOT:
                            three_times(g + 2)
                        if more > 1 and (t, m) == COPY_SLOT:
                            copy_fields(g + 2)
                        if m == GRAM_AT and at_least(T, 2):
                            copy_gram(T - 2)

            dims_outside(0, 0, 0)
            three_times(0)
            copy_fields(0)
            dims_outside(1, 0, 1)
            three_times(1)
            high_part(0, 0)
            copy_fields(1)
            period(0, 0, 0, 2)
            period(1, 0, 1, 2)
            with act.Fori(1, GROUPS // 2 - 1) as it:
                period(it * 2, it, 0, 2)
                period(it * 2 + 1, it, 1, 2)
            period(GROUPS - 2, GROUPS // 2 - 1, 0, 1)
            period(GROUPS - 1, GROUPS // 2 - 1, 1, 0)
            copy_gram(NT - 2)
            copy_gram(NT - 1)

            act.wait_ge(ctx_turned, 1)
            act.activation(dctxt, pt[0:CTX, :], ACT.Copy).then_inc(z_ready, 1)
            act.wait_ge(z0_ready, GROUPS)
            act.wait_ge(pool_summed, NT * N_POOL_SUM)
            act.wait_ge(tail_summed, NT * N_TAIL)
            act.activation(z0s[:, :], z0raw[:, :], ACT.Identity, bias=b0s[:, :]).then_inc(z_ready, 1)
            act.wait_ge(z2_done, 1)
            act.activation(z2s[:, :], p0[:, :], ACT.Identity, bias=b2s[:, :]).then_inc(z_ready, 1)
            for c in range(TOP1 // P):
                act.wait_ge(h1_done, c + 1)
                act.activation(h1[c][:, :], yb[c][:, :], ACT.Relu, bias=bt1[:, c:c + 1]).then_inc(h1_ready, 1)
            for c in range(TOP2 // P):
                act.wait_ge(h2_done, c + 1)
                act.activation(h2[c][:, :], (pt, pg)[c][:, :], ACT.Relu, bias=bt2[:, c:c + 1]).then_inc(h2_ready, 1)
            act.wait_ge(y_done, 1)
            act.activation(yrow, p0[0:1, :], ACT.Copy).then_inc(y_ready, 1)

        @block.vector
        def _(dve):
            dve.wait_ge(weights_in, 32)
            step = FIELDS + 1

            def cut(at, n):
                return w0raw[:, at:at + step * (n - 1) + 1:step]

            for s in range(HALF + 1):
                at = (s % CHUNKS) * ROWS + (s // CHUNKS) * FIELDS
                n = FIELDS - s
                if s == 0:
                    dve.tensor_copy(w0sym[:, at:at + FIELDS], cut(0, FIELDS)).then_inc(w0_sym, 1)
                else:
                    dve.tensor_tensor(w0sym[:, at:at + n], cut(s, n), cut(FIELDS * s, n), ALU.add).then_inc(w0_sym, 1)
                    dve.tensor_tensor(w0sym[:, at + n:at + FIELDS], cut(step * n + s - FIELDS, s),
                                      cut(step * n + FIELDS * (s - FIELDS), s), ALU.add).then_inc(w0_sym, 1)
            for n in range(W0_BANKS, TURNS):
                k = n - W0_BANKS
                j = 4 * (k % W_BANKS)
                w = min(4, FIELDS - j) * HID
                dve.wait_ge(w_turned, n + 1)
                if k < W_BANKS:
                    dve.wait_ge(w_hi, n + 1)
                    dve.tensor_tensor(w1l[:, j * HID:j * HID + w], yb[n % RING][:, 0:w],
                                      w1h[:, j * HID:j * HID + w].bitcast(F32), ALU.subtract).then_inc(w_lo, 1)
                else:
                    dve.tensor_copy(w2t[:, j:j + w // HID, :].rearrange("p j h -> p (j h)"),
                                    yb[n % RING][:, 0:w]).then_inc(w_lo, 1)

            def pair_chunk(g, c):
                rows = ROWS if c < CHUNKS - 1 else LAST_ROWS
                if c == 0:
                    dve.wait_ge(x0r_ready, g + 1)
                if c in (0, EARLY):
                    dve.wait_ge(rolled_in[c // EARLY], (g + 1) * (16 * REPS))
                dve.tensor_tensor(pairs[0:rows, c, :], pairs[0:rows, c, :], x0r[0:rows, :],
                                  ALU.mult).then_inc(pairs_ready, 1)

            def low_part(g, u):
                dve.wait_ge(x1h_ready, g + 1)
                dve.scalar_tensor_tensor(out=x1l[u][:, :], in0=p0[:, :], scalar=b0c[:, :],
                                         in1=x1h[u][:, :].bitcast(F32), op0=ALU.add,
                                         op1=ALU.subtract).then_inc(x1l_ready, 1)

            def sum_dims(g):
                dve.wait_ge(l0_done, g + 1)
                dve.tensor_reduce(z0raw[:, bass.ds(g * GROUP_B, GROUP_B)],
                                  p0[:, :].rearrange("p (b d) -> p b d", d=DIM), AX.X,
                                  ALU.add).then_inc(z0_ready, 1)

            def scale(g, t, u, m):
                T = g * TILES + t
                n = fields_of(m)
                if t == 0 and m == DVE_SCALES[0]:
                    dve.wait_ge(x0t_in[u], (g + 2 - u) * (8 * TILES))
                dve.wait_ge(bank_ready, T * BANKS + m + 1)
                if at_least(T, 1):
                    wait_product_free(dve, T - 1, m)
                dve.tensor_tensor(prod[m][:, 0:n * HID].rearrange("p (j h) -> p j h", h=HID),
                                  yb[m % RING][:, 0:n * HID].rearrange("p (j h) -> p j h", h=HID),
                                  x0t[u][:, t, BANK_F * m:BANK_F * m + n, None].to_broadcast([P, n, HID]),
                                  ALU.mult).then_inc(dve_scaled, 1)

            def chain_sum(T, p, k):
                acc = acc_d[p]
                for m in DVE_SUMS[k]:
                    wait_scaled(dve, T, m)
                if k == 0:
                    if at_least(T, 2):
                        dve.wait_ge(tail_summed, (T - 1) * N_TAIL)
                    a, b = (prod[m][:, :] for m in DVE_SUMS[0])
                    dve.tensor_tensor(acc[:, :], a, b, ALU.add).then_inc(chain_summed, 1)
                else:
                    dve.wait_ge(chain_summed, T * N_CHAIN + k)
                    dve.tensor_tensor(acc[:, :], acc[:, :], prod[DVE_SUMS[k][0]][:, :],
                                      ALU.add).then_inc(chain_summed, 1)

            def tail_sum(T, p, k):
                acc = acc_d[p]
                if k == 0:
                    dve.wait_ge(chain_summed, (T + 1) * N_CHAIN)
                    wait_scaled(dve, T, BANKS - 1)
                    dve.tensor_tensor(acc[:, :], acc[:, :], prod[BANKS - 1][:, :], ALU.add).then_inc(tail_summed, 1)
                    return
                dve.wait_ge(tail_summed, T * N_TAIL + k)
                if k == 1:
                    dve.wait_ge(pool_summed, (T + 1) * N_POOL_SUM)
                    dve.tensor_tensor(acc[:, :], acc[:, :], acc_p[p][:, :], ALU.add).then_inc(tail_summed, 1)
                elif k == 2:
                    dve.tensor_tensor(acc[:, 0:2 * HID], acc[:, 0:2 * HID], acc[:, 2 * HID:4 * HID],
                                      ALU.add).then_inc(tail_summed, 1)
                else:
                    if at_least(T, 2):
                        dve.wait_ge(gram_done, T - 1)
                    dve.tensor_tensor(x2t[p][:, :], acc[:, 0:HID], acc[:, HID:2 * HID],
                                      ALU.add).then_inc(tail_summed, 1)

            def period(g, u, more):
                for t in range(TILES):
                    T = g * TILES + t
                    for m in range(BANKS):
                        if m in DVE_SCALES:
                            scale(g, t, u, m)
                        if m == LAST_CHAIN_AT and at_least(T, 1):
                            chain_sum(T - 1, (t + 1) % 2, N_CHAIN - 1)
                        if m in CHAIN_AT:
                            chain_sum(T, t % 2, CHAIN_AT[m])
                        if m in TAIL_AT and at_least(T, 1):
                            tail_sum(T - 1, (t + 1) % 2, TAIL_AT[m])
                        if more and (t, m) in PAIR_SLOTS:
                            pair_chunk(g + 1, PAIR_SLOTS.index((t, m)))
                        if more and (t, m) == LOW_SLOT:
                            low_part(g + 1, 1 - u)
                        if more and (t, m) == Z0_SLOT:
                            sum_dims(g + 1)

            for c in range(CHUNKS):
                pair_chunk(0, c)
            low_part(0, 0)
            sum_dims(0)
            dve.wait_ge(b1_in, 16)
            period(0, 0, True)
            period(1, 1, True)
            with dve.Fori(1, GROUPS // 2 - 1) as it:
                period(it * 2, 0, True)
                period(it * 2 + 1, 1, True)
            period(GROUPS - 2, 0, True)
            period(GROUPS - 1, 1, False)
            chain_sum(NT - 1, (NT - 1) % 2, N_CHAIN - 1)
            for k in range(N_TAIL):
                tail_sum(NT - 1, (NT - 1) % 2, k)

        @block.tensor
        def _(pe):
            pe.wait_ge(consts, 9)
            pe.wait_ge(w0_sym, 2 * HALF + 1)

            def wait_bank(n):
                if n < W0_BANKS + RING:
                    if n >= RING:
                        pe.wait_ge(w_hi, n - RING + 1)
                else:
                    pe.wait_ge(w_lo, n - RING - W0_BANKS + 1)

            for n in range(TURNS):
                if n >= RING:
                    wait_bank(n)
                if n == W0_BANKS + W_BANKS:
                    pe.wait_ge(w2_in, 16)
                if n < W0_BANKS:
                    for i in range(4 * n, min(4 * n + 4, CHUNKS)):
                        rows = ROWS if i < CHUNKS - 1 else LAST_ROWS
                        op = pe.transpose(yb[n % RING][0:rows, (i % 4) * HID:(i % 4 + 1) * HID],
                                          w0sym[:, i * ROWS:i * ROWS + rows], ident[:, :])
                else:
                    raw = w1raw if n < W0_BANKS + W_BANKS else w2raw
                    j0 = 4 * ((n - W0_BANKS) % W_BANKS)
                    for j in range(j0, min(j0 + 4, FIELDS)):
                        op = pe.transpose(yb[n % RING][:, (j - j0) * HID:(j - j0 + 1) * HID],
                                          raw[:, j * HID:(j + 1) * HID], ident[:, :])
                op.then_inc(w_turned, 1)

            def turn_fields(g):
                pe.wait_ge(x0t3_ready, g + 1)
                if at_least(g, 1):
                    pe.wait_ge(x0r_ready, g)
                for t in range(TILES):
                    op = pe.transpose(pt[0:ROWS, t * P:(t + 1) * P], x0t3[:, t, :], ident[:, :])
                op.then_inc(x0_turned, 1)

            def layer0(g, c):
                if c == 0 and at_least(g, 1):
                    pe.wait_ge(x1h_ready, g)
                    pe.wait_ge(x1l_ready, g)
                    pe.wait_ge(z0_ready, g)
                rows = ROWS if c < CHUNKS - 1 else LAST_ROWS
                pe.wait_ge(pairs_ready, g * CHUNKS + c + 1)
                op = pe.matmul(p0[:, :], w0t[0:rows, c, :], pairs[0:rows, c, :],
                               start=(c == 0), stop=(c == CHUNKS - 1))
                if c == CHUNKS - 1:
                    op.then_inc(l0_done, 1)

            def gram_product(T, p):
                pe.wait_ge(tail_summed, (T + 1) * N_TAIL)
                pe.wait_ge(bdiag_ready, (T + 1) * N_DVE)
                if at_least(T, 1):
                    pe.wait_ge(gram_copied, T)
                pe.matmul(pg[:, 0:TILE_B * GRAM], x2t[p][:, :],
                          bdiag[p][:, :, :].rearrange("p b c -> p (b c)"),
                          start=True, stop=True).then_inc(gram_done, 1)

            def layer1_bank(g, t, u, m):
                T = g * TILES + t
                if m >= RING:
                    wait_scaled(pe, T, m - RING)
                elif at_least(T, 1):
                    wait_scaled(pe, T - 1, m + BANKS - RING)
                w = fields_of(m) * HID
                at = BANK_F * m * HID
                cols = slice(t * P, (t + 1) * P)
                hi, lo = x1h[u][:, cols], x1l[u][:, cols]
                pe.matmul(yb[m % RING][:, 0:w], hi, w1h[:, at:at + w], start=True, stop=False)
                pe.matmul(yb[m % RING][:, 0:w], hi, w1l[:, at:at + w], start=False, stop=False)
                pe.matmul(yb[m % RING][:, 0:w], lo, w1h[:, at:at + w], start=False,
                          stop=True).then_inc(bank_ready, 1)

            def period(g, u, more):
                pe.wait_ge(x1h_ready, g + 1)
                pe.wait_ge(x1l_ready, g + 1)
                for t in range(TILES):
                    T = g * TILES + t
                    for m in range(BANKS):
                        layer1_bank(g, t, u, m)
                        if m == GRAM_AT and at_least(T, 2):
                            gram_product(T - 2, t % 2)
                        if (t, m) == TURN_SLOT and more > 1:
                            turn_fields(g + 2)
                        if (t, m) in LAYER0_SLOTS and more > 0:
                            layer0(g + 1, LAYER0_SLOTS.index((t, m)))

            turn_fields(0)
            pe.wait_ge(w_hi, W0_BANKS)
            for c in range(CHUNKS):
                layer0(0, c)
            turn_fields(1)
            pe.wait_ge(w_hi, W0_BANKS + W_BANKS)
            pe.wait_ge(w_lo, 2 * W_BANKS)
            period(0, 0, 2)
            period(1, 1, 2)
            with pe.Fori(1, GROUPS // 2 - 1) as it:
                period(it * 2, 0, 2)
                period(it * 2 + 1, 1, 2)
            period(GROUPS - 2, 0, 1)
            period(GROUPS - 1, 1, 0)
            pe.wait_ge(small_in, 16 * 6)
            pe.wait_ge(x0r_ready, GROUPS)
            for c in range(BATCH // P):
                op = pe.transpose(pt[0:CTX, c * P:(c + 1) * P], dctx[:, c, :], ident[:, :])
            op.then_inc(ctx_turned, 1)
            gram_product(NT - 2, 0)
            gram_product(NT - 1, 1)
            pe.wait_ge(gram_copied, NT)
            for j in range(FIELDS):
                op = pe.matmul(p0[:, :], w2t[:, j, :], gram[:, j, :], start=(j == 0), stop=(j == FIELDS - 1))
            op.then_inc(z2_done, 1)
            pe.wait_ge(z_ready, 2)
            pe.wait_ge(dense_in, 16 * 3)
            for c in range(TOP1 // P):
                wait_scaled(pe, NT - 1, BANKS - RING + c)
                cols = slice(c * P, (c + 1) * P)
                pe.matmul(yb[c][:, :], wt1[:, 0, cols], z0s[:, :], start=True, stop=False)
                pe.matmul(yb[c][:, :], wt1[:, 1, cols], gram[:, FIELDS, :], start=False, stop=False)
                pe.matmul(yb[c][:, :], wt1c[:, cols], dctxt, start=False, stop=False)
            pe.wait_ge(z_ready, 3)
            for c in range(TOP1 // P):
                pe.matmul(yb[c][:, :], wt1[:, 2, c * P:(c + 1) * P], z2s[:, :], start=False,
                          stop=True).then_inc(h1_done, 1)
            for c in range(TOP1 // P):
                pe.wait_ge(h1_ready, c + 1)
                for o in range(TOP2 // P):
                    op = pe.matmul((pt, pg)[o][:, :], wt2[:, c, o * P:(o + 1) * P], h1[c][:, :],
                                   start=(c == 0), stop=(c == TOP1 // P - 1))
                    if c == TOP1 // P - 1:
                        op.then_inc(h2_done, 1)
            for c in range(TOP2 // P):
                pe.wait_ge(h2_ready, c + 1)
                op = pe.matmul(p0[0:1, :], wt3[:, c:c + 1], h2[c][:, :], start=(c == 0), stop=(c == TOP2 // P - 1))
            op.then_inc(y_done, 1)


_REST = ["W_top1", "b_top1", "W_top2", "b_top2", "W_top3", "L0_rec_W0", "L0_rec_b0",
         "L0_rec_W1", "L0_rec_b1", "L0_rec_W2", "L0_rec_b2"]


def kernel(**inputs):
    import numpy as _np
    import concourse.bacc as _bacc
    from concourse import mybir as _mybir
    from concourse.bass_utils import run_bass_kernel_spmd as _run

    nc = _bacc.Bacc("TRN2", target_bir_lowering=False, num_devices=1,
                     dynamic_dma_scratch_size=8192)
    arrays, aps = {}, {}
    tables = [_np.asarray(inputs[f"tbl_{j}"]) for j in range(FIELDS)]
    begins = [0]
    for t in tables[:-1]:
        begins.append(begins[-1] + t.shape[0])
    begins += [0] * (COLS - FIELDS)
    laid = {"table": _np.concatenate(tables, axis=0),
            "bases": _np.repeat(_np.array(begins, _np.int32).reshape(QUARTERS, PER_Q), GROUP_B, axis=0)}
    for name in ["dense_ctx", "ids", "table", "bases"] + _REST:
        a = _np.ascontiguousarray(laid[name] if name in laid else inputs[name])
        arrays[f"in_{name}_dram"] = a
        aps[name] = nc.dram_tensor(f"in_{name}_dram", a.shape, _mybir.dt.from_np(a.dtype),
                                   kind="ExternalInput").ap()
    out = nc.dram_tensor("out_0_dram", (BATCH, 1), _mybir.dt.float32, kind="ExternalOutput").ap()
    tower(nc, aps["dense_ctx"], aps["ids"], aps["table"], aps["bases"], *[aps[n] for n in _REST], out)
    r = _run(nc, [arrays], core_ids=[0])
    return r.results[0]["out_0_dram"]
```

```python
from contextlib import ExitStack

import concourse.bass as bass
from concourse import mybir

F32 = mybir.dt.float32
F32R = mybir.dt.float32r
I32 = mybir.dt.int32
ALU = mybir.AluOpType
ACT = mybir.ActivationFunctionType
AX = mybir.AxisListType

P = 128
BATCH, FIELDS, DIM, HID = 512, 39, 16, 128
CTX = 16
TOP1, TOP2 = 512, 256

TILE_B = P // DIM
TILES = 4
GROUP_B = TILE_B * TILES
GROUP_N = P * TILES
GROUPS = BATCH // GROUP_B
NT = GROUPS * TILES

QUARTERS = P // GROUP_B
PER_Q = -(-FIELDS // QUARTERS)
SHORT_Q = FIELDS - PER_Q * (QUARTERS - 1)
COLS = QUARTERS * PER_Q

REPS, CHUNKS = 3, 7
ROWS = REPS * FIELDS
LAST_ROWS = 2 * FIELDS
HALF = (FIELDS - 1) // 2

BANK_F = 4
BANKS = -(-FIELDS // BANK_F)
LAST_F = FIELDS - BANK_F * (BANKS - 1)
RING = 5
GRAM = FIELDS + 1

ACT_SCALES = (1, 2, 4, 5, 7, 8, 9)
DVE_SCALES = (0, 3, 6)
POOL_SUMS = ((1, 2), (4,), (7,))
DVE_SUMS = (5, 8)
TWICE = (1, 2, 4)
N_ACT, N_DVE = len(ACT_SCALES), len(DVE_SCALES)
N_POOL_SUM, N_CHAIN, N_TAIL = len(POOL_SUMS), len(DVE_SUMS), 6


SUMS_AT = {0: (("last chain", 1),),
           3: (("tail", 0),),
           5: (("tail", 1),),
           6: (("tail", 2),),
           7: (("chain", 0), ("tail", 3)),
           8: (("tail", 4),),
           9: (("tail", 5),)}
GRAM_AT = 3

PAIR_SLOTS = ((0, 6), (0, 9), (1, 3), (1, 6), (1, 9), (2, 3), (2, 6))
LAYER0_SLOTS = ((1, 3), (1, 6), (1, 9), (2, 2), (2, 5), (2, 8), (3, 1))
HIGH_SLOT = (3, 2)
LOW_SLOT = (3, 4)
Z0_SLOT = (3, 9)
DIMS_SLOT = (0, 3)
THREE_SLOT = (1, 9)
TURN_SLOT = (3, 3)
COPY_SLOT = (3, 4)
WARM = 24
DIMS_TURN = 7
EARLY = 3

PLAIN = 8
SPLIT_RING = 4


def fields_of(m):
    return BANK_F if m < BANKS - 1 else LAST_F


def tower(nc, dense_ctx, ids, table, bases, W_top1, b_top1, W_top2, b_top2, W_top3,
          W0, b0, W1, b1, W2, b2, out):
    ctx = ExitStack()
    with ctx:
        def sb(name, shape, dt=F32):
            return ctx.enter_context(nc.sbuf_tensor(name, shape, dt))

        def pb(name):
            return ctx.enter_context(nc.psum_tensor(name, [P, 512], F32))

        def sem(name):
            return ctx.enter_context(nc.semaphore(name))

        ident = sb("ident", [P, P])
        mask = sb("mask", [P, TILE_B])
        ids_all = sb("ids_all", [P, GROUPS, PER_Q], I32)
        one = sb("one", [P, 1])
        base = sb("base", [P, PER_Q], I32)
        idx = [sb(f"idx{u}", [P, PER_Q], I32) for u in range(2)]
        emb = [sb(f"emb{u}", [P, PER_Q, DIM]) for u in range(2)]
        embq = [sb(f"embq{u}", [P, DIM, PER_Q]) for u in range(2)]
        embt = sb("embt", [2 * GROUP_B, DIM, COLS])
        x0t = [sb(f"x0t{u}", [P, TILES, COLS]) for u in range(2)]
        x0a = sb("x0a", [P, TILES, COLS])
        x0t3 = sb("x0t3", [P, TILES, ROWS])
        x0r = sb("x0r", [ROWS, GROUP_N])
        late = sb("late", [P, CHUNKS * GROUP_N])
        x1h = [sb(f"x1h{u}", [P, GROUP_N], F32R) for u in range(2)]
        x1l = [sb(f"x1l{u}", [P, GROUP_N], F32R) for u in range(2)]
        w0t = sb("w0t", [ROWS, CHUNKS, HID])
        w1h = sb("w1h", [P, FIELDS * HID], F32R)
        w1l = sb("w1l", [P, FIELDS * HID], F32R)
        w2t = sb("w2t", [P, FIELDS, HID])
        prod = {m: [sb(f"prod{m}_{u}", [P, BANK_F * HID]) for u in range(2 if m in TWICE else 1)]
                for m in ACT_SCALES}
        acc_d = [sb(f"acc_d{u}", [P, BANK_F * HID]) for u in range(2)]
        acc_p = [sb(f"acc_p{u}", [P, BANK_F * HID]) for u in range(2)]
        x2h = [sb(f"x2h{u}", [P, HID], F32R) for u in range(2)]
        x2l = [sb(f"x2l{u}", [P, HID], F32R) for u in range(2)]
        x0h = sb("x0h", [P, TILES, COLS], F32R)
        x0l = sb("x0l", [P, TILES, COLS])
        bdiag_h = [sb(f"bdiag_h{u}", [P, TILE_B, GRAM], F32R) for u in range(2)]
        bdiag_l = [sb(f"bdiag_l{u}", [P, TILE_B, GRAM], F32R) for u in range(2)]
        gram = sb("gram", [P, GRAM, BATCH])
        z0raw = sb("z0raw", [P, BATCH])
        b0c = sb("b0c", [P, 1])
        b2c = sb("b2c", [P, 1])
        b0s = sb("b0s", [P, 1])
        b2s = sb("b2s", [P, 1])
        wt3 = sb("wt3", [P, TOP2 // P])
        bt1 = sb("bt1", [P, TOP1 // P])
        bt2 = sb("bt2", [P, TOP2 // P])
        dctx = sb("dctx", [P, BATCH // P, CTX])
        yrow = x0r[0:1, :]

        flat = gram[:, :, :].rearrange("p c b -> p (c b)")
        w1raw = flat[:, 0:FIELDS * HID]
        w2raw = flat[:, 5120:5120 + FIELDS * HID]
        w0raw = flat[:, 10240:10240 + FIELDS * FIELDS]
        w0sym = flat[:, 12288:12288 + CHUNKS * ROWS]
        pairs = late[0:ROWS, :].rearrange("p (c n) -> p c n", c=CHUNKS)
        wt1 = late[:, 0:3 * TOP1].rearrange("p (c n) -> p c n", c=3)
        wt2 = late[:, 3 * TOP1:3 * TOP1 + TOP1 // P * TOP2].rearrange("p (c n) -> p c n", n=TOP2)
        wt1c = late[0:CTX, 5 * GROUP_N:6 * GROUP_N]
        dctxt = late[0:CTX, 6 * GROUP_N:7 * GROUP_N]
        spare = [b for m in ACT_SCALES for b in prod[m]]
        z0s, z2s = spare[0:2]
        h1 = spare[2:2 + TOP1 // P]
        h2 = spare[2 + TOP1 // P:2 + TOP1 // P + TOP2 // P]

        w2h, w2l = w1h, w1l
        gram_h = [b[:, :] for b in x1h] + [w1h[:, i * BATCH:(i + 1) * BATCH] for i in range(SPLIT_RING - 2)]
        gram_l = [b[:, :] for b in x1l] + [w1l[:, i * BATCH:(i + 1) * BATCH] for i in range(SPLIT_RING - 2)]

        x0d = nc.dram_tensor("x0_scratch", [2, 2 * FIELDS, GROUP_N], F32, kind="Internal").ap()

        yb = [pb(f"yb{i}") for i in range(RING)]
        p0 = pb("p0")
        pt = pb("pt")
        pg = pb("pg")

        ids_in = sem("ids_in")
        idx_ready = sem("idx_ready")
        gathered = [sem(f"gathered{u}") for u in range(2)]
        embq_ready = sem("embq_ready")
        embt_in = sem("embt_in")
        w0_in = sem("w0_in")
        w1_in = sem("w1_in")
        w2_in = [sem(f"w2_in{h}") for h in range(2)]
        small_in = sem("small_in")
        b1_in = sem("b1_in")
        dense_in = sem("dense_in")
        consts = sem("consts")
        w0_sym = sem("w0_sym")
        w_turned = sem("w_turned")
        w_hi = sem("w_hi")
        w_lo = sem("w_lo")
        sp_waited = sem("sp_waited")
        x0a_in = sem("x0a_in")
        x0t_in = [sem(f"x0t_in{u}") for u in range(2)]
        x0t3_ready = sem("x0t3_ready")
        x0_turned = sem("x0_turned")
        x0r_ready = sem("x0r_ready")
        x0d_out = sem("x0d_out")
        rolled_in = [sem(f"rolled_in{h}") for h in range(2)]
        pairs_ready = sem("pairs_ready")
        l0_done = sem("l0_done")
        x1h_ready = sem("x1h_ready")
        x1l_ready = sem("x1l_ready")
        z0_ready = sem("z0_ready")
        bank_ready = sem("bank_ready")
        act_scaled = sem("act_scaled")
        dve_scaled = sem("dve_scaled")
        pool_summed = sem("pool_summed")
        chain_summed = sem("chain_summed")
        tail_summed = sem("tail_summed")
        x0_split = sem("x0_split")
        bdiag_ready = sem("bdiag_ready")
        gram_done = sem("gram_done")
        gram_copied = sem("gram_copied")
        w2_high = sem("w2_high")
        w2_low = sem("w2_low")
        gram_high = sem("gram_high")
        gram_low = sem("gram_low")
        gram_used = sem("gram_used")
        z2_done = sem("z2_done")
        z_ready = sem("z_ready")
        ctx_turned = sem("ctx_turned")
        bias_ready = sem("bias_ready")
        h1_done = sem("h1_done")
        h1_ready = sem("h1_ready")
        h2_done = sem("h2_done")
        h2_ready = sem("h2_ready")
        y_done = sem("y_done")
        y_ready = sem("y_ready")
        y_out = sem("y_out")

        def wait_scaled(eng, T, m):
            if m in ACT_SCALES:
                eng.wait_ge(act_scaled, T * N_ACT + ACT_SCALES.index(m) + 1)
            else:
                eng.wait_ge(dve_scaled, T * N_DVE + DVE_SCALES.index(m) + 1)

        def wait_product_free(eng, T, m):
            back = 2 if m in TWICE else 1
            if not at_least(T, back):
                return
            T = T - back
            for k, ms in enumerate(POOL_SUMS):
                if m in ms:
                    eng.wait_ge(pool_summed, T * N_POOL_SUM + k + 1)
            if m in DVE_SUMS:
                eng.wait_ge(chain_summed, T * N_CHAIN + DVE_SUMS.index(m) + 1)
            if m == BANKS - 1:
                eng.wait_ge(tail_summed, T * N_TAIL + 1)

        def product(m, t):
            return prod[m][t % len(prod[m])]

        def at_least(T, n):
            return not isinstance(T, int) or T >= n

        W_BANKS = -(-FIELDS // 4)
        W0_BANKS = -(-CHUNKS // 4)
        TURNS = W0_BANKS + 2 * W_BANKS
        W2_HALF = W_BANKS // 2
        W2_CUT = W2_HALF * 4 * HID

        def split_weights(b):
            j = PLAIN + 4 * b
            return j * HID, min(j + 4, FIELDS) * HID

        W2_SPLITS = -(-(FIELDS - PLAIN) // 4)
        w2flat = w2t[:, :, :].rearrange("p j h -> p (j h)")

        block = ctx.enter_context(nc.Block())

        @block.sync
        def _(sp):
            sp.dma_start(base[:, :], bases).then_inc(ids_in, 16)
            sp.dma_start(ids_all[:, :, :], ids).then_inc(ids_in, 16)
            sp.dma_start(w0raw, W0).then_inc(w0_in, 16)
            sp.dma_start(w1raw, W1).then_inc(w1_in, 16)
            sp.dma_start(dctx[:, :, :], dense_ctx.rearrange("(c p) n -> p c n", p=P)).then_inc(small_in, 16)
            with nc.allow_non_contiguous_dma(reason="a few bias columns"):
                sp.dma_start(wt3[:, :], W_top3.rearrange("(c p) n -> p (c n)", p=P)).then_inc(small_in, 16)
                sp.dma_start(bt1[:, :], b_top1.rearrange("(c p) -> p c", p=P)).then_inc(small_in, 16)
                sp.dma_start(bt2[:, :], b_top2.rearrange("(c p) -> p c", p=P)).then_inc(small_in, 16)

            def samples(g, u):
                for h in range(QUARTERS):
                    sp.dma_start(embt[u * GROUP_B:(u + 1) * GROUP_B, :, h * PER_Q:(h + 1) * PER_Q],
                                 embq[u][h * GROUP_B:(h + 1) * GROUP_B, :, :]).then_inc(embt_in, 16)

            def columns(dst, g, u, done):
                for t in range(TILES):
                    b = u * GROUP_B + t * TILE_B
                    sp.dma_start(dst[:, t, :], embt[b:b + TILE_B, :, :]).then_inc(done, 16)

            def store_fields(g, u):
                sp.wait_ge(x0r_ready, g + 1)
                sp.dma_start(x0d[u, :, :], x0r[0:2 * FIELDS, :]).then_inc(x0d_out, 16)

            def load_rolled(g, u):
                sp.wait_ge(x0d_out, (g + 1) * 16)
                for h, (c0, c1) in enumerate(((0, EARLY), (EARLY, CHUNKS))):
                    for q in range(REPS):
                        n = c1 - c0 - (1 if q == REPS - 1 and c1 == CHUNKS else 0)
                        first = x0d[u, c0 + CHUNKS * q:c0 + CHUNKS * q + FIELDS, :]
                        row = first.ap[0][0]
                        src = bass.AP(first.tensor, first.offset, [[row, FIELDS], [row, n], [1, GROUP_N]])
                        sp.dma_start(pairs[q * FIELDS:(q + 1) * FIELDS, c0:c0 + n, :], src).then_inc(rolled_in[h], 16)

            def early_columns(g, u):
                if at_least(g, 1):
                    sp.wait_ge(x0t3_ready, g)
                    sp.sem_inc(sp_waited, 1)
                sp.wait_ge(embt_in, (g + 1) * (16 * QUARTERS))
                columns(x0a, g, u, x0a_in)

            def prepare(g, u):
                sp.wait_ge(embq_ready, g + 1)
                samples(g, u)
                early_columns(g, u)
                store_fields(g, u)
                load_rolled(g, u)

            def period(g, u, more=2):
                if more > 0:
                    if at_least(g, 1):
                        sp.wait_ge(act_scaled, g * (TILES * N_ACT))
                        sp.sem_inc(sp_waited, 1)
                        sp.wait_ge(dve_scaled, g * (TILES * N_DVE))
                        sp.wait_ge(bdiag_ready, g * (TILES * N_DVE))
                    columns(x0t[1 - u], g + 1, 1 - u, x0t_in[1 - u])
                if more > 1:
                    prepare(g + 2, u)

            def load_w2(h):
                w = slice(h * W2_CUT, (h + 1) * W2_CUT if h == 0 else FIELDS * HID)
                sp.dma_start(w2raw[:, w], W2[:, w]).then_inc(w2_in[h], 16)

            sp.wait_ge(embq_ready, 1)
            samples(0, 0)
            load_w2(0)
            early_columns(0, 0)
            load_w2(1)
            store_fields(0, 0)
            sp.wait_ge(embq_ready, 2)
            samples(1, 1)
            load_rolled(0, 0)
            columns(x0t[0], 0, 0, x0t_in[0])
            early_columns(1, 1)
            store_fields(1, 1)
            load_rolled(1, 1)
            period(0, 0)
            period(1, 1)
            with sp.Fori(1, GROUPS // 2 - 1) as it:
                period(it * 2, 0)
                period(it * 2 + 1, 1)
            period(GROUPS - 2, 0, 1)
            sp.wait_ge(l0_done, GROUPS)
            sp.dma_start(wt1, W_top1[0:3 * P, :].rearrange("(c p) n -> p c n", p=P)).then_inc(dense_in, 16)
            sp.dma_start(wt1c, W_top1[3 * P:3 * P + CTX, :]).then_inc(dense_in, 16)
            sp.dma_start(wt2, W_top2.rearrange("(c p) n -> p c n", p=P)).then_inc(dense_in, 16)
            sp.wait_ge(y_ready, 1)
            sp.dma_start(out.rearrange("b n -> n b"), yrow).then_inc(y_out, 16)
            sp.wait_ge(y_out, 16)

        @block.gpsimd
        def _(pool):
            def rows_of(g, u):
                pool.tensor_tensor(idx[u][:, 0:SHORT_Q], ids_all[:, g, 0:SHORT_Q] if isinstance(g, int) else
                                   ids_all[:, bass.ds(g, 1), 0:SHORT_Q].rearrange("p g i -> p (g i)"),
                                   base[:, 0:SHORT_Q], ALU.add).then_inc(idx_ready, 1)
                n = (QUARTERS - 1) * GROUP_B
                pool.tensor_tensor(idx[u][0:n, SHORT_Q:PER_Q], ids_all[0:n, g, SHORT_Q:PER_Q] if isinstance(g, int) else
                                   ids_all[0:n, bass.ds(g, 1), SHORT_Q:PER_Q].rearrange("p g i -> p (g i)"),
                                   base[0:n, SHORT_Q:PER_Q], ALU.add).then_inc(idx_ready, 1)

            def gather(u, i):
                n = P if i < SHORT_Q else (QUARTERS - 1) * GROUP_B
                pool.indirect_dma_start(emb[u][0:n, i, :], None, table[:, :],
                                        bass.IndirectOffsetOnAxis(idx[u][0:n, i:i + 1], 0)).then_inc(gathered[u], 16)

            pool.memset(ident[:, :], 1.0).then_inc(consts, 1)
            pool.memset(mask[:, :], 1.0).then_inc(consts, 1)
            pool.memset(one[:, :], 1.0).then_inc(consts, 1)
            pool.wait_ge(consts, 1)
            pool.affine_select(out=ident[:, :], in_=ident[:, :], compare_op=ALU.is_equal, fill=0.0,
                               base=0, pattern=[[-1, P]], channel_multiplier=1).then_inc(consts, 1)
            pool.wait_ge(consts, 4)
            pool.affine_select(out=mask[:, :], in_=mask[:, :], compare_op=ALU.is_ge, fill=0.0,
                               base=0, pattern=[[-DIM, TILE_B]], channel_multiplier=1).then_inc(consts, 1)
            pool.wait_ge(consts, 5)
            pool.affine_select(out=mask[:, :], in_=mask[:, :], compare_op=ALU.is_ge, fill=0.0,
                               base=DIM - 1, pattern=[[DIM, TILE_B]], channel_multiplier=-1).then_inc(consts, 1)
            pool.wait_ge(consts, 6)
            for u in range(2):
                pool.tensor_copy(bdiag_h[u][:, :, FIELDS], mask[:, :]).then_inc(consts, 1)
                pool.tensor_tensor(bdiag_l[u][:, :, FIELDS], mask[:, :], mask[:, :], ALU.subtract).then_inc(consts, 1)

            for u in range(2):
                pool.memset(emb[u][:, :, :], 0.0).then_inc(consts, 1)
            pool.wait_ge(consts, 12)
            pool.wait_ge(ids_in, 16 * 2)
            for u in range(2):
                rows_of(u, u)
                pool.wait_ge(idx_ready, 2 * (u + 1))
                for i in range(PER_Q):
                    gather(u, i)
            pool.wait_ge(embq_ready, 1)
            rows_of(2, 0)
            pool.wait_ge(idx_ready, 2 * 3)
            for i in range(PER_Q):
                gather(0, i)

            def tile(g, t, u):
                T = g * TILES + t
                if at_least(T, 2):
                    pool.wait_ge(gram_done, T - 1)
                for part, dst in ((x0h[:, :, :].bitcast(F32), bdiag_h), (x0l, bdiag_l)):
                    op = pool.tensor_tensor(dst[t % 2][:, :, 0:FIELDS],
                                            mask[:, :, None].to_broadcast([P, TILE_B, FIELDS]),
                                            part[:, t, None, 0:FIELDS].to_broadcast([P, TILE_B, FIELDS]),
                                            ALU.mult)
                op.then_inc(bdiag_ready, N_DVE)

            def sums(g, t, k):
                T = g * TILES + t
                acc = acc_p[t % 2]
                for m in POOL_SUMS[k]:
                    wait_scaled(pool, T, m)
                if k == 0:
                    if at_least(T, 2):
                        pool.wait_ge(tail_summed, (T - 2) * N_TAIL + 2)
                    a, b = (product(m, t)[:, :] for m in POOL_SUMS[0])
                    pool.tensor_tensor(acc[:, :], a, b, ALU.add).then_inc(pool_summed, 1)
                else:
                    pool.wait_ge(pool_summed, T * N_POOL_SUM + k)
                    pool.tensor_tensor(acc[:, :], acc[:, :], product(POOL_SUMS[k][0], t)[:, :],
                                       ALU.add).then_inc(pool_summed, 1)

            def period(g, u, more):
                todo = list(range(PER_Q)) if more else []
                if more:
                    pool.wait_ge(embq_ready, g + 2)
                pool.wait_ge(x0t_in[u], (g + 2 - u) * (8 * TILES))
                if at_least(g, 1):
                    pool.wait_ge(bdiag_ready, g * (TILES * N_DVE))
                pool.tensor_tensor(x0h[:, :, :], x0t[u][:, :, :], one[:, :, None].to_broadcast([P, TILES, COLS]),
                                   ALU.mult).then_inc(x0_split, 1)
                pool.wait_ge(x0_split, 2 * g + 1)
                pool.tensor_tensor(x0l[:, :, :], x0t[u][:, :, :], x0h[:, :, :].bitcast(F32),
                                   ALU.subtract).then_inc(x0_split, 1)
                pool.wait_ge(x0_split, 2 * g + 2)
                for t in range(TILES):
                    tile(g, t, u)
                    if more and t == 0:
                        rows_of(g + 3, 1 - u)
                        pool.wait_ge(idx_ready, 2 * (g + 4))
                    for s in range(N_POOL_SUM):
                        sums(g, t, s)
                        if todo:
                            gather(1 - u, todo.pop(0))

            period(0, 0, True)
            with pool.Fori(0, GROUPS // 2 - 2) as it:
                period(it * 2 + 1, 1, True)
                period(it * 2 + 2, 0, True)
            period(GROUPS - 3, 1, False)
            period(GROUPS - 2, 0, False)
            period(GROUPS - 1, 1, False)
            for b in range(W2_SPLITS):
                lo, hi = split_weights(b)
                pool.wait_ge(w2_high, b + 1)
                pool.tensor_tensor(w2l[:, lo:hi], w2flat[:, lo:hi], w2h[:, lo:hi].bitcast(F32),
                                   ALU.subtract).then_inc(w2_low, 1)

        @block.scalar
        def _(act):
            act.wait_ge(ids_in, 16 * 2)
            with nc.allow_non_contiguous_dma(reason="a few bias columns"):
                act.dma_start(b0c[:, :], b0.rearrange("(p n) -> p n", n=1)).then_inc(small_in, 16)
                act.dma_start(b2c[:, :], b2.rearrange("(p n) -> p n", n=1)).then_inc(small_in, 16)
            act.dma_start(product(BANKS - 1, 0)[:, LAST_F * HID:BANK_F * HID],
                          b1.rearrange("(a h) -> a h", a=1).to_broadcast([P, HID])).then_inc(b1_in, 16)

            def copy_weights(n):
                act.wait_ge(w_turned, n + 1)
                if n < W0_BANKS:
                    for i in range(4 * n, min(4 * n + 4, CHUNKS)):
                        rows = ROWS if i < CHUNKS - 1 else LAST_ROWS
                        op = act.activation(w0t[0:rows, i, :], yb[n % RING][0:rows, (i % 4) * HID:(i % 4 + 1) * HID], ACT.Copy)
                    op.then_inc(w_hi, 1)
                else:
                    j = 4 * (n - W0_BANKS)
                    w = min(4, FIELDS - j) * HID
                    act.activation(w1h[:, j * HID:j * HID + w], yb[n % RING][:, 0:w], ACT.Copy).then_inc(w_hi, 1)

            def copy_fields(g):
                act.wait_ge(x0_turned, g + 1)
                if at_least(g, 1):
                    act.wait_ge(pairs_ready, g * CHUNKS)
                act.activation(x0r[:, :], pt[0:ROWS, :], ACT.Copy).then_inc(x0r_ready, 1)

            def dims_outside(g, half_g, u):
                act.wait_ge(gathered[u], (half_g + 1) * (16 * PER_Q))
                if at_least(g, 2):
                    act.wait_ge(embt_in, (g - 1) * (16 * QUARTERS))
                act.activation(embq[u][:, :, :], emb[u][:, :, :].rearrange("p i d -> p d i"),
                               ACT.Copy).then_inc(embq_ready, 1)

            def three_times(g):
                act.wait_ge(x0a_in, (g + 1) * (16 * TILES))
                if at_least(g, 1):
                    act.wait_ge(x0_turned, g)
                act.activation(x0t3[:, :, :].rearrange("p t (r j) -> p t r j", r=REPS),
                               x0a[:, :, None, 0:FIELDS].to_broadcast([P, TILES, REPS, FIELDS]),
                               ACT.Copy).then_inc(x0t3_ready, 1)

            def high_part(g, u):
                act.wait_ge(l0_done, g + 1)
                if at_least(g, 2):
                    act.wait_ge(bank_ready, (g - 1) * (TILES * BANKS))
                act.activation(x1h[u][:, :], p0[:, :], ACT.Identity, bias=b0c[:, :]).then_inc(x1h_ready, 1)

            def copy_gram(T):
                act.wait_ge(gram_done, T + 1)
                act.activation(gram[:, :, bass.ds(T * TILE_B, TILE_B)],
                               pg[:, 0:TILE_B * GRAM].rearrange("p (b c) -> p c b", c=GRAM),
                               ACT.Copy).then_inc(gram_copied, 1)

            def scale(g, t, u, m):
                T = g * TILES + t
                if t == 0 and m == ACT_SCALES[0]:
                    act.wait_ge(x0t_in[u], (g + 2 - u) * (8 * TILES))
                act.wait_ge(bank_ready, T * BANKS + m + 1)
                wait_product_free(act, T, m)
                for i in range(fields_of(m)):
                    j = BANK_F * m + i
                    op = act.activation(product(m, t)[:, i * HID:(i + 1) * HID], yb[m % RING][:, i * HID:(i + 1) * HID],
                                        ACT.Copy, scale=x0t[u][:, t, j:j + 1])
                op.then_inc(act_scaled, 1)

            def period(g, half_g, u, more):
                for t in range(TILES):
                    T = g * TILES + t
                    for m in range(BANKS):
                        if m in ACT_SCALES:
                            scale(g, t, u, m)
                        if more > 0 and (t, m) == HIGH_SLOT:
                            high_part(g + 1, 1 - u)
                        if more > 1 and (t, m) == DIMS_SLOT:
                            dims_outside(g + 2, half_g + 1, u)
                        if more > 1 and (t, m) == THREE_SLOT:
                            three_times(g + 2)
                        if more > 1 and (t, m) == COPY_SLOT:
                            copy_fields(g + 2)
                        if m == GRAM_AT and at_least(T, 2):
                            copy_gram(T - 2)

            for n in range(W0_BANKS):
                copy_weights(n)
            for n in range(W0_BANKS, W0_BANKS + W_BANKS):
                if n == DIMS_TURN:
                    dims_outside(0, 0, 0)
                copy_weights(n)
            three_times(0)
            dims_outside(1, 0, 1)
            copy_fields(0)
            act.wait_ge(small_in, 16 * 6)
            act.activation(b0s[:, :], b0c[:, :], ACT.Copy, scale=float(DIM)).then_inc(bias_ready, 1)
            act.activation(b2s[:, :], b2c[:, :], ACT.Copy, scale=float(DIM)).then_inc(bias_ready, 1)
            three_times(1)
            high_part(0, 0)
            copy_fields(1)
            period(0, 0, 0, 2)
            period(1, 0, 1, 2)
            with act.Fori(1, GROUPS // 2 - 1) as it:
                period(it * 2, it, 0, 2)
                period(it * 2 + 1, it, 1, 2)
            period(GROUPS - 2, GROUPS // 2 - 1, 0, 1)
            period(GROUPS - 1, GROUPS // 2 - 1, 1, 0)
            def w2_high_part(b):
                lo, hi = split_weights(b)
                if b == 0:
                    act.wait_ge(bank_ready, NT * BANKS)
                act.activation(w2h[:, lo:hi], w2flat[:, lo:hi], ACT.Copy).then_inc(w2_high, 1)

            def gram_high_part(i):
                r = i % SPLIT_RING
                if i == 0:
                    act.wait_ge(gram_copied, NT)
                if i >= SPLIT_RING:
                    act.wait_ge(gram_used, i - SPLIT_RING + 1)
                act.activation(gram_h[r], gram[:, PLAIN + i, :], ACT.Copy).then_inc(gram_high, 1)

            copy_gram(NT - 2)
            for b in range(W2_SPLITS // 2):
                w2_high_part(b)
            copy_gram(NT - 1)
            for i in range(FIELDS - PLAIN):
                gram_high_part(i)
                if 1 <= i <= W2_SPLITS - W2_SPLITS // 2:
                    w2_high_part(W2_SPLITS // 2 + i - 1)
                if i == 2 * SPLIT_RING:
                    act.wait_ge(ctx_turned, 1)
                    act.activation(dctxt, pt[0:CTX, :], ACT.Copy).then_inc(z_ready, 1)
                    act.wait_ge(z0_ready, GROUPS)
                    act.wait_ge(pool_summed, NT * N_POOL_SUM)
                    act.wait_ge(tail_summed, NT * N_TAIL)
                    act.activation(z0s[:, :], z0raw[:, :], ACT.Identity, bias=b0s[:, :]).then_inc(z_ready, 1)

            act.wait_ge(z2_done, 1)
            act.activation(z2s[:, :], p0[:, :], ACT.Identity, bias=b2s[:, :]).then_inc(z_ready, 1)
            for c in range(TOP1 // P):
                act.wait_ge(h1_done, c + 1)
                act.activation(h1[c][:, :], yb[c][:, :], ACT.Relu, bias=bt1[:, c:c + 1]).then_inc(h1_ready, 1)
            for c in range(TOP2 // P):
                act.wait_ge(h2_done, c + 1)
                act.activation(h2[c][:, :], (pt, pg)[c][:, :], ACT.Relu, bias=bt2[:, c:c + 1]).then_inc(h2_ready, 1)
            act.wait_ge(y_done, 1)
            act.activation(yrow, p0[0:1, :], ACT.Copy).then_inc(y_ready, 1)

        @block.vector
        def _(dve):
            dve.wait_ge(w0_in, 16)
            step = FIELDS + 1

            def cut(at, n):
                return w0raw[:, at:at + step * (n - 1) + 1:step]

            for s in range(HALF + 1):
                at = (s % CHUNKS) * ROWS + (s // CHUNKS) * FIELDS
                n = FIELDS - s
                if s == 0:
                    dve.tensor_copy(w0sym[:, at:at + FIELDS], cut(0, FIELDS)).then_inc(w0_sym, 1)
                else:
                    dve.tensor_tensor(w0sym[:, at:at + n], cut(s, n), cut(FIELDS * s, n), ALU.add).then_inc(w0_sym, 1)
                    dve.tensor_tensor(w0sym[:, at + n:at + FIELDS], cut(step * n + s - FIELDS, s),
                                      cut(step * n + FIELDS * (s - FIELDS), s), ALU.add).then_inc(w0_sym, 1)
            def low_weights(n):
                k = n - W0_BANKS
                j = 4 * (k % W_BANKS)
                w = min(4, FIELDS - j) * HID
                dve.wait_ge(w_turned, n + 1)
                if k < W_BANKS:
                    dve.wait_ge(w_hi, n + 1)
                    dve.tensor_tensor(w1l[:, j * HID:j * HID + w], yb[n % RING][:, 0:w],
                                      w1h[:, j * HID:j * HID + w].bitcast(F32), ALU.subtract).then_inc(w_lo, 1)
                else:
                    dve.tensor_copy(w2t[:, j:j + w // HID, :].rearrange("p j h -> p (j h)"),
                                    yb[n % RING][:, 0:w]).then_inc(w_lo, 1)

            def pair_chunk(g, c):
                rows = ROWS if c < CHUNKS - 1 else LAST_ROWS
                if c == 0:
                    dve.wait_ge(x0r_ready, g + 1)
                if c in (0, EARLY):
                    dve.wait_ge(rolled_in[c // EARLY], (g + 1) * (16 * REPS))
                dve.tensor_tensor(pairs[0:rows, c, :], pairs[0:rows, c, :], x0r[0:rows, :],
                                  ALU.mult).then_inc(pairs_ready, 1)

            def low_part(g, u):
                dve.wait_ge(x1h_ready, g + 1)
                dve.scalar_tensor_tensor(out=x1l[u][:, :], in0=p0[:, :], scalar=b0c[:, :],
                                         in1=x1h[u][:, :].bitcast(F32), op0=ALU.add,
                                         op1=ALU.subtract).then_inc(x1l_ready, 1)

            def sum_dims(g):
                dve.wait_ge(l0_done, g + 1)
                dve.tensor_reduce(z0raw[:, bass.ds(g * GROUP_B, GROUP_B)],
                                  p0[:, :].rearrange("p (b d) -> p b d", d=DIM), AX.X,
                                  ALU.add).then_inc(z0_ready, 1)

            def scale(g, t, u, m):
                T = g * TILES + t
                n = fields_of(m)
                if t == 0 and m == DVE_SCALES[0]:
                    dve.wait_ge(x0t_in[u], (g + 2 - u) * (8 * TILES))
                dve.wait_ge(bank_ready, T * BANKS + m + 1)
                acc = acc_d[t % 2]
                if m == DVE_SCALES[0]:
                    if at_least(T, 2):
                        dve.wait_ge(tail_summed, (T - 1) * N_TAIL)
                    dve.tensor_tensor(acc[:, :].rearrange("p (j h) -> p j h", h=HID),
                                      yb[m % RING][:, :].rearrange("p (j h) -> p j h", h=HID),
                                      x0t[u][:, t, BANK_F * m:BANK_F * (m + 1), None].to_broadcast([P, BANK_F, HID]),
                                      ALU.mult).then_inc(dve_scaled, 1)
                    return
                dve.wait_ge(dve_scaled, T * N_DVE + DVE_SCALES.index(m))
                for i in range(BANK_F):
                    j = BANK_F * m + i
                    part = acc[:, i * HID:(i + 1) * HID]
                    op = dve.scalar_tensor_tensor(out=part, in0=yb[m % RING][:, i * HID:(i + 1) * HID],
                                                  scalar=x0t[u][:, t, j:j + 1], in1=part,
                                                  op0=ALU.mult, op1=ALU.add)
                op.then_inc(dve_scaled, 1)

            def chain_sum(T, p, k):
                m = DVE_SUMS[k]
                if k == 0:
                    dve.wait_ge(dve_scaled, (T + 1) * N_DVE)
                else:
                    dve.wait_ge(chain_summed, T * N_CHAIN + k)
                wait_scaled(dve, T, m)
                dve.tensor_tensor(acc_d[p][:, :], acc_d[p][:, :], product(m, p)[:, :],
                                  ALU.add).then_inc(chain_summed, 1)

            def tail_sum(T, p, k):
                acc = acc_d[p]
                if k == 0:
                    dve.wait_ge(chain_summed, (T + 1) * N_CHAIN)
                    wait_scaled(dve, T, BANKS - 1)
                    dve.tensor_tensor(acc[:, :], acc[:, :], product(BANKS - 1, p)[:, :], ALU.add).then_inc(tail_summed, 1)
                    return
                dve.wait_ge(tail_summed, T * N_TAIL + k)
                if k == 1:
                    dve.wait_ge(pool_summed, (T + 1) * N_POOL_SUM)
                    dve.tensor_tensor(acc[:, :], acc[:, :], acc_p[p][:, :], ALU.add).then_inc(tail_summed, 1)
                elif k == 2:
                    dve.tensor_tensor(acc[:, 0:2 * HID], acc[:, 0:2 * HID], acc[:, 2 * HID:4 * HID],
                                      ALU.add).then_inc(tail_summed, 1)
                elif k == 3:
                    if at_least(T, 2):
                        dve.wait_ge(gram_done, T - 1)
                    dve.tensor_tensor(x2h[p][:, :], acc[:, 0:HID], acc[:, HID:2 * HID],
                                      ALU.add).then_inc(tail_summed, 1)
                elif k == 4:
                    dve.tensor_tensor(acc[:, 0:HID], acc[:, 0:HID], acc[:, HID:2 * HID],
                                      ALU.add).then_inc(tail_summed, 1)
                else:
                    dve.tensor_tensor(x2l[p][:, :], acc[:, 0:HID], x2h[p][:, :].bitcast(F32),
                                      ALU.subtract).then_inc(tail_summed, 1)

            def period(g, u, more):
                for t in range(TILES):
                    T = g * TILES + t
                    for m in range(BANKS):
                        if m in DVE_SCALES:
                            scale(g, t, u, m)
                        for kind, k in SUMS_AT.get(m, ()):
                            if kind == "chain":
                                chain_sum(T, t % 2, k)
                            elif at_least(T, 1):
                                (tail_sum if kind == "tail" else chain_sum)(T - 1, (t + 1) % 2, k)
                        if more and (t, m) in PAIR_SLOTS:
                            pair_chunk(g + 1, PAIR_SLOTS.index((t, m)))
                        if more and (t, m) == LOW_SLOT:
                            low_part(g + 1, 1 - u)
                        if more and (t, m) == Z0_SLOT:
                            sum_dims(g + 1)

            for n in range(W0_BANKS, TURNS):
                low_weights(n)
            for c in range(CHUNKS):
                pair_chunk(0, c)
            low_part(0, 0)
            sum_dims(0)
            dve.wait_ge(b1_in, 16)
            period(0, 0, True)
            period(1, 1, True)
            with dve.Fori(1, GROUPS // 2 - 1) as it:
                period(it * 2, 0, True)
                period(it * 2 + 1, 1, True)
            period(GROUPS - 2, 0, True)
            period(GROUPS - 1, 1, False)
            chain_sum(NT - 1, (NT - 1) % 2, N_CHAIN - 1)
            for k in range(N_TAIL):
                tail_sum(NT - 1, (NT - 1) % 2, k)
            for i in range(FIELDS - PLAIN):
                r = i % SPLIT_RING
                if i >= SPLIT_RING:
                    dve.wait_ge(gram_used, i - SPLIT_RING + 1)
                dve.wait_ge(gram_high, i + 1)
                dve.tensor_tensor(gram_l[r], gram[:, PLAIN + i, :], gram_h[r].bitcast(F32),
                                  ALU.subtract).then_inc(gram_low, 1)

        @block.tensor
        def _(pe):
            pe.wait_ge(consts, 10)
            pe.wait_ge(w0_sym, 2 * HALF + 1)

            def wait_bank(n):
                if n < W0_BANKS + RING:
                    if n >= RING:
                        pe.wait_ge(w_hi, n - RING + 1)
                else:
                    pe.wait_ge(w_lo, n - RING - W0_BANKS + 1)

            def turn_weights(n):
                if n >= RING:
                    wait_bank(n)
                if n == W0_BANKS:
                    pe.wait_ge(w1_in, 16)
                for h in range(2):
                    if n == W0_BANKS + W_BANKS + h * W2_HALF:
                        pe.wait_ge(w2_in[h], 16)
                if n < W0_BANKS:
                    for i in range(4 * n, min(4 * n + 4, CHUNKS)):
                        rows = ROWS if i < CHUNKS - 1 else LAST_ROWS
                        op = pe.transpose(yb[n % RING][0:rows, (i % 4) * HID:(i % 4 + 1) * HID],
                                          w0sym[:, i * ROWS:i * ROWS + rows], ident[:, :])
                else:
                    raw = w1raw if n < W0_BANKS + W_BANKS else w2raw
                    j0 = 4 * ((n - W0_BANKS) % W_BANKS)
                    for j in range(j0, min(j0 + 4, FIELDS)):
                        op = pe.transpose(yb[n % RING][:, (j - j0) * HID:(j - j0 + 1) * HID],
                                          raw[:, j * HID:(j + 1) * HID], ident[:, :])
                op.then_inc(w_turned, 1)

            def turn_fields(g):
                pe.wait_ge(x0t3_ready, g + 1)
                if at_least(g, 1):
                    pe.wait_ge(x0r_ready, g)
                for t in range(TILES):
                    op = pe.transpose(pt[0:ROWS, t * P:(t + 1) * P], x0t3[:, t, :], ident[:, :])
                op.then_inc(x0_turned, 1)

            def layer0(g, c):
                if c == 0 and at_least(g, 1):
                    pe.wait_ge(x1h_ready, g)
                    pe.wait_ge(x1l_ready, g)
                    pe.wait_ge(z0_ready, g)
                rows = ROWS if c < CHUNKS - 1 else LAST_ROWS
                pe.wait_ge(pairs_ready, g * CHUNKS + c + 1)
                op = pe.matmul(p0[:, :], w0t[0:rows, c, :], pairs[0:rows, c, :],
                               start=(c == 0), stop=(c == CHUNKS - 1))
                if c == CHUNKS - 1:
                    op.then_inc(l0_done, 1)

            def gram_product(T, p):
                pe.wait_ge(tail_summed, (T + 1) * N_TAIL)
                pe.wait_ge(bdiag_ready, (T + 1) * N_DVE)
                if at_least(T, 1):
                    pe.wait_ge(gram_copied, T)
                high, low = (b[p][:, :, :].rearrange("p b c -> p (b c)") for b in (bdiag_h, bdiag_l))
                pe.matmul(pg[:, 0:TILE_B * GRAM], x2h[p][:, :], high, start=True, stop=False)
                pe.matmul(pg[:, 0:TILE_B * GRAM], x2h[p][:, :], low, start=False, stop=False)
                pe.matmul(pg[:, 0:TILE_B * GRAM], x2l[p][:, :], high, start=False, stop=True).then_inc(gram_done, 1)

            def layer1_bank(g, t, u, m):
                T = g * TILES + t
                if m >= RING:
                    wait_scaled(pe, T, m - RING)
                elif at_least(T, 1):
                    wait_scaled(pe, T - 1, m + BANKS - RING)
                w = fields_of(m) * HID
                at = BANK_F * m * HID
                cols = slice(t * P, (t + 1) * P)
                hi, lo = x1h[u][:, cols], x1l[u][:, cols]
                pe.matmul(yb[m % RING][:, 0:w], hi, w1h[:, at:at + w], start=True, stop=False)
                pe.matmul(yb[m % RING][:, 0:w], hi, w1l[:, at:at + w], start=False, stop=False)
                pe.matmul(yb[m % RING][:, 0:w], lo, w1h[:, at:at + w], start=False,
                          stop=True).then_inc(bank_ready, 1)

            def period(g, u, more):
                pe.wait_ge(x1h_ready, g + 1)
                pe.wait_ge(x1l_ready, g + 1)
                for t in range(TILES):
                    T = g * TILES + t
                    for m in range(BANKS):
                        layer1_bank(g, t, u, m)
                        if m == GRAM_AT and at_least(T, 2):
                            gram_product(T - 2, t % 2)
                        if (t, m) == TURN_SLOT and more > 1:
                            turn_fields(g + 2)
                        if (t, m) in LAYER0_SLOTS and more > 0:
                            layer0(g + 1, LAYER0_SLOTS.index((t, m)))

            for n in range(W0_BANKS + W_BANKS):
                turn_weights(n)
            turn_fields(0)
            for n in range(W0_BANKS + W_BANKS, TURNS):
                turn_weights(n)
            for i in range(WARM):
                pe.transpose(p0[:, 0:P], ident[:, :], ident[:, :])
            pe.wait_ge(w_hi, W0_BANKS)
            for c in range(CHUNKS):
                layer0(0, c)
            turn_fields(1)
            pe.wait_ge(w_hi, W0_BANKS + W_BANKS)
            pe.wait_ge(w_lo, 2 * W_BANKS)
            period(0, 0, 2)
            period(1, 1, 2)
            with pe.Fori(1, GROUPS // 2 - 1) as it:
                period(it * 2, 0, 2)
                period(it * 2 + 1, 1, 2)
            period(GROUPS - 2, 0, 1)
            period(GROUPS - 1, 1, 0)
            pe.wait_ge(small_in, 16 * 6)
            pe.wait_ge(x0r_ready, GROUPS)
            for c in range(BATCH // P):
                op = pe.transpose(pt[0:CTX, c * P:(c + 1) * P], dctx[:, c, :], ident[:, :])
            op.then_inc(ctx_turned, 1)
            gram_product(NT - 2, 0)

            def layer2_plain(h):
                cols = slice(h * BATCH // 2, (h + 1) * BATCH // 2)
                for j in range(PLAIN):
                    pe.matmul(p0[:, cols], w2t[:, j, :], gram[:, j, cols], start=(h == 0 and j == 0), stop=False)

            pe.wait_ge(gram_copied, NT // 2)
            layer2_plain(0)
            gram_product(NT - 1, 1)
            pe.wait_ge(gram_copied, NT)
            layer2_plain(1)
            for i in range(FIELDS - PLAIN):
                r, j = i % SPLIT_RING, PLAIN + i
                w = slice(j * HID, (j + 1) * HID)
                pe.wait_ge(w2_high, i // 4 + 1)
                pe.wait_ge(gram_high, i + 1)
                pe.matmul(p0[:, :], w2h[:, w], gram_h[r], start=False, stop=False)
                pe.wait_ge(w2_low, i // 4 + 1)
                pe.matmul(p0[:, :], w2l[:, w], gram_h[r], start=False, stop=False)
                pe.wait_ge(gram_low, i + 1)
                op = pe.matmul(p0[:, :], w2h[:, w], gram_l[r], start=False, stop=(j == FIELDS - 1))
                op.then_inc(z2_done if j == FIELDS - 1 else gram_used, 1)
            pe.wait_ge(z_ready, 2)
            pe.wait_ge(dense_in, 16 * 3)
            for c in range(TOP1 // P):
                wait_scaled(pe, NT - 1, BANKS - RING + c)
                cols = slice(c * P, (c + 1) * P)
                pe.matmul(yb[c][:, :], wt1[:, 0, cols], z0s[:, :], start=True, stop=False)
                pe.matmul(yb[c][:, :], wt1[:, 1, cols], gram[:, FIELDS, :], start=False, stop=False)
                pe.matmul(yb[c][:, :], wt1c[:, cols], dctxt, start=False, stop=False)
            pe.wait_ge(z_ready, 3)
            for c in range(TOP1 // P):
                pe.matmul(yb[c][:, :], wt1[:, 2, c * P:(c + 1) * P], z2s[:, :], start=False,
                          stop=True).then_inc(h1_done, 1)
            for c in range(TOP1 // P):
                pe.wait_ge(h1_ready, c + 1)
                for o in range(TOP2 // P):
                    op = pe.matmul((pt, pg)[o][:, :], wt2[:, c, o * P:(o + 1) * P], h1[c][:, :],
                                   start=(c == 0), stop=(c == TOP1 // P - 1))
                    if c == TOP1 // P - 1:
                        op.then_inc(h2_done, 1)
            for c in range(TOP2 // P):
                pe.wait_ge(h2_ready, c + 1)
                op = pe.matmul(p0[0:1, :], wt3[:, c:c + 1], h2[c][:, :], start=(c == 0), stop=(c == TOP2 // P - 1))
            op.then_inc(y_done, 1)


_REST = ["W_top1", "b_top1", "W_top2", "b_top2", "W_top3", "L0_rec_W0", "L0_rec_b0",
         "L0_rec_W1", "L0_rec_b1", "L0_rec_W2", "L0_rec_b2"]


def kernel(**inputs):
    import numpy as _np
    import concourse.bacc as _bacc
    from concourse import mybir as _mybir
    from concourse.bass_utils import run_bass_kernel_spmd as _run

    nc = _bacc.Bacc("TRN2", target_bir_lowering=False, num_devices=1,
                     dynamic_dma_scratch_size=8192)
    arrays, aps = {}, {}
    tables = [_np.asarray(inputs[f"tbl_{j}"]) for j in range(FIELDS)]
    begins = [0]
    for t in tables[:-1]:
        begins.append(begins[-1] + t.shape[0])
    begins += [0] * (COLS - FIELDS)
    laid = {"table": _np.concatenate(tables, axis=0),
            "bases": _np.repeat(_np.array(begins, _np.int32).reshape(QUARTERS, PER_Q), GROUP_B, axis=0)}
    given = _np.asarray(inputs["ids"])
    ids = _np.zeros((BATCH, COLS), given.dtype)
    ids[:, :FIELDS] = given
    laid["ids"] = ids.reshape(GROUPS, GROUP_B, QUARTERS, PER_Q).transpose(2, 1, 0, 3).reshape(P, GROUPS, PER_Q)
    for name in ["dense_ctx", "ids", "table", "bases"] + _REST:
        a = _np.ascontiguousarray(laid[name] if name in laid else inputs[name])
        arrays[f"in_{name}_dram"] = a
        aps[name] = nc.dram_tensor(f"in_{name}_dram", a.shape, _mybir.dt.from_np(a.dtype),
                                   kind="ExternalInput").ap()
    out = nc.dram_tensor("out_0_dram", (BATCH, 1), _mybir.dt.float32, kind="ExternalOutput").ap()
    tower(nc, aps["dense_ctx"], aps["ids"], aps["table"], aps["bases"], *[aps[n] for n in _REST], out)
    r = _run(nc, [arrays], core_ids=[0])
    return r.results[0]["out_0_dram"]
```
